# Optimizing a Trainium2 kernel written in Bass

```python
import numpy as np
import jax
import jax.numpy as jnp

def _softmax(x, axis=-1):
    return jax.nn.softmax(x, axis=axis)

def _gelu(x):
    return jax.nn.gelu(x, approximate=True)

def _silu(x):
    return jax.nn.silu(x)

def _sigmoid(x):
    return jax.nn.sigmoid(x)

def _layernorm(x, axis=-1, eps=1e-05):
    m = jnp.mean(x, axis=axis, keepdims=True)
    v = jnp.var(x, axis=axis, keepdims=True)
    return (x - m) / jnp.sqrt(v + eps)

def _scatter_add(tgt, idx, src, axis=0):
    return tgt.at[idx].add(src)

def _segment_sum(src, seg, n):
    return jax.ops.segment_sum(src, seg, n)
kernel_name = 'mk_seq_preln_d1_jaxref_r8_9956cf'

def setup_inputs(seed: int=0):
    np.random.seed(seed)
    _w = jnp.asarray

    def _L0_attn_setup():
        import jax, jax.numpy as jnp
        import numpy as np
        NUM_HEADS = 16
        EPS = 1e-06

        def _split_heads(t, h):
            b, s, d = t.shape
            return t.reshape(b, s, h, d // h).transpose(0, 2, 1, 3)
        key = jax.random.key(seed)
        ks = jax.random.split(key, 6)
        b, s, d = (4, 512, 128)
        scale = 1.0 / np.sqrt(d)
        return {'x': jax.random.normal(ks[0], (b, s, d), dtype=jnp.float32), 'wq': jax.random.normal(ks[1], (d, d), dtype=jnp.float32) * scale, 'wk': jax.random.normal(ks[2], (d, d), dtype=jnp.float32) * scale, 'wv': jax.random.normal(ks[3], (d, d), dtype=jnp.float32) * scale, 'wo': jax.random.normal(ks[4], (d, d), dtype=jnp.float32) * scale, 'bo': jnp.zeros((d,), dtype=jnp.float32)}
    _L0_attn_in = _L0_attn_setup()

    def _L0_ffn_setup():
        import jax, jax.numpy as jnp
        import numpy as np
        D_MODEL = 128
        N_EXPERTS = 16
        TOP_K = 2
        EXPERT_DIM = 128
        SHARED_DIM = 256
        B, T = (2, 128)
        key = jax.random.key(seed)
        ks = jax.random.split(key, 7)
        std = 0.02
        return {'x': jax.random.normal(ks[0], (B, T, D_MODEL), dtype=jnp.float32), 'router_w': jax.random.normal(ks[1], (N_EXPERTS, D_MODEL), dtype=jnp.float32) * std, 'gate_up_w': jax.random.normal(ks[2], (N_EXPERTS, D_MODEL, 2 * EXPERT_DIM), dtype=jnp.float32) * std, 'down_w': jax.random.normal(ks[3], (N_EXPERTS, EXPERT_DIM, D_MODEL), dtype=jnp.float32) * std, 'shared_gate_w': jax.random.normal(ks[4], (SHARED_DIM, D_MODEL), dtype=jnp.float32) * std, 'shared_up_w': jax.random.normal(ks[5], (SHARED_DIM, D_MODEL), dtype=jnp.float32) * std, 'shared_down_w': jax.random.normal(ks[6], (D_MODEL, SHARED_DIM), dtype=jnp.float32) * std}
    _L0_ffn_in = _L0_ffn_setup()
    _d = {'L0_attn_x': _L0_attn_in['x'], 'L0_attn_wq': _L0_attn_in['wq'], 'L0_attn_wk': _L0_attn_in['wk'], 'L0_attn_wv': _L0_attn_in['wv'], 'L0_attn_wo': _L0_attn_in['wo'], 'L0_attn_bo': _L0_attn_in['bo'], 'L0_ffn_router_w': _L0_ffn_in['router_w'], 'L0_ffn_gate_up_w': _L0_ffn_in['gate_up_w'], 'L0_ffn_down_w': _L0_ffn_in['down_w'], 'L0_ffn_shared_gate_w': _L0_ffn_in['shared_gate_w'], 'L0_ffn_shared_up_w': _L0_ffn_in['shared_up_w'], 'L0_ffn_shared_down_w': _L0_ffn_in['shared_down_w']}
    _x0 = _d['L0_attn_x']
    _d['L0_attn_x'] = jax.random.normal(jax.random.fold_in(jax.random.key(seed), 1), (16, 256, 128), dtype=_x0.dtype)
    del _x0
    return _d

def reference(L0_attn_x, L0_attn_wq, L0_attn_wk, L0_attn_wv, L0_attn_wo, L0_attn_bo, L0_ffn_router_w, L0_ffn_gate_up_w, L0_ffn_down_w, L0_ffn_shared_gate_w, L0_ffn_shared_up_w, L0_ffn_shared_down_w):

    def _L0_attn_ref(x, wq, wk, wv, wo, bo):
        import jax, jax.numpy as jnp
        import numpy as np
        NUM_HEADS = 16
        EPS = 1e-06

        def _split_heads(t, h):
            b, s, d = t.shape
            return t.reshape(b, s, h, d // h).transpose(0, 2, 1, 3)
        h = NUM_HEADS
        q = _split_heads(x @ wq.T, h)
        k = _split_heads(x @ wk.T, h)
        v = _split_heads(x @ wv.T, h)
        qf = jax.nn.elu(q) + 1.0
        kf = jax.nn.elu(k) + 1.0
        k_sum = jnp.sum(kf, axis=-2)
        denom = jnp.sum(qf * k_sum[:, :, None, :], axis=-1, keepdims=True) + EPS
        kv = jnp.einsum('bhsd,bhse->bhde', kf, v)
        q_kv = jnp.einsum('bhsd,bhde->bhse', qf, kv)
        out = q_kv / denom
        b, _, s, dh = out.shape
        out = out.transpose(0, 2, 1, 3).reshape(b, s, h * dh)
        return out @ wo.T + bo

    def _L0_ffn_ref(x, router_w, gate_up_w, down_w, shared_gate_w, shared_up_w, shared_down_w):
        import jax, jax.numpy as jnp
        import numpy as np
        D_MODEL = 128
        N_EXPERTS = 16
        TOP_K = 2
        EXPERT_DIM = 128
        SHARED_DIM = 256
        B, T = (2, 128)
        Bb, Tt, C = x.shape
        N = Bb * Tt
        E = gate_up_w.shape[0]
        logits = jnp.einsum('btc,ec->bte', x, router_w)
        top_vals, top_idx = jax.lax.top_k(logits, TOP_K)
        gates = jax.nn.sigmoid(top_vals)
        xf = x.reshape(N, C)
        sel = top_idx.reshape(N, TOP_K)
        gw = gates.reshape(N, TOP_K)
        w_full = jnp.zeros((N, E), dtype=x.dtype).at[jnp.arange(N)[:, None], sel].add(gw)
        gu = jnp.einsum('nc,ech->neh', xf, gate_up_w)
        gate, up = jnp.split(gu, 2, axis=-1)
        h = jax.nn.silu(gate) * up
        out_all = jnp.einsum('neh,ehc->nec', h, down_w)
        moe = jnp.einsum('ne,nec->nc', w_full, out_all).reshape(Bb, Tt, C)
        sg = jnp.einsum('btc,sc->bts', x, shared_gate_w)
        su = jnp.einsum('btc,sc->bts', x, shared_up_w)
        shared = jnp.einsum('bts,cs->btc', jax.nn.silu(sg) * su, shared_down_w)
        return moe + shared
    x = L0_attn_x
    x = x + _L0_attn_ref(_layernorm(x, axis=-1), L0_attn_wq, L0_attn_wk, L0_attn_wv, L0_attn_wo, L0_attn_bo)
    x = x + _L0_ffn_ref(_layernorm(x, axis=-1), L0_ffn_router_w, L0_ffn_gate_up_w, L0_ffn_down_w, L0_ffn_shared_gate_w, L0_ffn_shared_up_w, L0_ffn_shared_down_w)
    return x

_drawn_inputs = setup_inputs


def setup_inputs(seed=0):
    import zlib

    import numpy as np

    out = dict(_drawn_inputs(seed))
    spreads = {'L0_attn_bo': (0.0, 0.1)}
    factors = {'L0_attn_wq': 3.425,
     'L0_ffn_router_w': 8.0,
     'L0_ffn_gate_up_w': 8.0,
     'L0_ffn_down_w': 8.0,
     'L0_ffn_shared_gate_w': 6.899,
     'L0_ffn_shared_up_w': 6.837,
     'L0_ffn_shared_down_w': 6.81}
    for name, (base, spread) in spreads.items():
        noise = np.random.default_rng([zlib.crc32(name.encode()), seed]).standard_normal(out[name].shape)
        drawn = base * np.exp(spread * noise) if base else spread * noise
        out[name] = jnp.asarray(drawn.astype(out[name].dtype))
    for name, factor in factors.items():
        out[name] = (out[name] * factor).astype(out[name].dtype)
    return out
```

```python
import concourse.bass as bass
from concourse import mybir
from contextlib import ExitStack

P = 128
D = 128
HEADS = 16
HD = D // HEADS
BATCHES, SEQ = 16, 256
TOKENS = BATCHES * SEQ
EXPERTS, TOP_K = 16, 2
EXP_DIM = 128
SHARED = 256
LN_EPS, ATT_EPS = 1e-5, 1e-6

QUAD = 4
QTOK = QUAD * P
NQ = TOKENS // QTOK
SPQ = QTOK // SEQ
RK = D + HEADS

REGION = TOKENS + P
REGION_BLOCKS = REGION // P
ROW = D + 2
SKIP = 1 << 20
PAIRS = TOP_K * TOKENS
MAX_BLOCKS = PAIRS // P + EXPERTS - 1
BODY = 10
TURNS = -(-MAX_BLOCKS // BODY)
BLOCKS = TURNS * BODY
HALF = 2 * P
HALVES = TOKENS // HALF

C_IDENT, C_TRI, C_MASK = 0, P, 2 * P
C_IOTA = C_MASK + RK
C_BASE = C_IOTA + EXPERTS
C_SLOT = C_BASE + EXPERTS
C_CUM = C_SLOT + 1
C_ALL = C_CUM + 2 * EXPERTS
W_Q, W_KV, W_O, W_R = 0, D, 3 * D, 4 * D
W_ALL = 4 * D + EXPERTS
F_GU = 0
F_DN = EXPERTS * 2 * EXP_DIM
F_SG = F_DN + EXPERTS * D
F_SU = F_SG + SHARED
F_SD = F_SU + SHARED
F_ALL = F_SD + SHARED // P * D


def preln_block(nc, x, w_att, bo, w_ffn, consts, tokid, out):
    F32, BF16 = mybir.dt.float32, mybir.dt.bfloat16
    U32, I32 = mybir.dt.uint32, mybir.dt.int32
    ALU, ACT, AX = mybir.AluOpType, mybir.ActivationFunctionType, mybir.AxisListType

    x_v = x.rearrange("(q b p j) c -> q p b (j c)", b=SPQ, p=P, j=2)
    out_v = out.rearrange("(q b p j) c -> q p b (j c)", b=SPQ, p=P, j=2)

    with ExitStack() as ctx:
        def sb(name, shape, dt=F32):
            return ctx.enter_context(nc.sbuf_tensor(name, shape, dt))

        def pb(name, shape):
            return ctx.enter_context(nc.psum_tensor(name, shape, F32))

        def sem(name):
            return ctx.enter_context(nc.semaphore(name))

        routed = nc.dram_tensor("routed", ((EXPERTS + 1) * REGION, ROW), F32, kind="Internal").ap()
        results = nc.dram_tensor("results", (PAIRS, D), F32, kind="Internal").ap()
        res_v = results.rearrange("(k q b p j) c -> k q p b (j c)", k=TOP_K, b=SPQ, p=P, j=2)

        X = sb("X", [P, NQ * QTOK])
        X1 = sb("X1", [P, NQ * QTOK])
        ZT = sb("ZT", [P, NQ * QTOK])
        WA = sb("WA", [P, W_ALL])
        WF = sb("WF", [P, F_ALL])
        CN = sb("CN", [P, C_ALL])
        TOK = sb("TOK", [P, NQ * QUAD * TOP_K], U32)
        bo_row = sb("bo_row", [1, D])
        bo_all = sb("bo_all", [P, D])
        ones_row = sb("ones_row", [1, P])
        ones = sb("ones", [P, P], BF16)
        tri = sb("tri", [P, P], BF16)
        eps = sb("eps", [P, 1])
        ident = CN[:, C_IDENT:C_IDENT + P]

        a_stat = sb("a_stat", [P, QUAD, 6])
        a_mv = sb("a_mv", [P, QUAD, 2])
        a_rs = sb("a_rs", [P, 6, QUAD])
        XN = sb("XN", [P, 2, QUAD, D])
        XNT = sb("XNT", [P, 2, QTOK])
        rq = sb("rq", [P, QTOK])
        eq = sb("eq", [P, QTOK])
        rk = sb("rk", [P, QUAD, D])
        ek = sb("ek", [P, QUAD, D])
        QF = sb("QF", [P, 2, QTOK])
        KF = sb("KF", [P, 2, QUAD, D])
        V = sb("V", [P, 2, QUAD, D + 4])
        KV = sb("KV", [P, SPQ, RK])
        den = sb("den", [P, QUAD, HEADS])
        rden = sb("rden", [P, QUAD, HEADS])
        att = sb("att", [P, QUAD, D])
        attT = sb("attT", [P, QTOK])
        c_stat = sb("c_stat", [P, QUAD, 6])
        c_mv = sb("c_mv", [P, QUAD, 2])
        c_rs = sb("c_rs", [P, 6, QUAD])
        Z = sb("Z", [P, 2, QUAD, TOP_K, ROW])
        zT = sb("zT", [P, QTOK])
        logits = sb("logits", [P, QUAD, EXPERTS])
        top = sb("top", [P, QUAD, 8])
        top_i = sb("top_i", [P, QUAD, 8], U32)
        top_f = sb("top_f", [P, QUAD, TOP_K])
        onehot = sb("onehot", [P, QUAD, TOP_K, EXPERTS])
        chosen = sb("chosen", [P, QUAD, EXPERTS], BF16)
        chosen_q = sb("chosen_q", [P, EXPERTS], BF16)
        chosen_all = sb("chosen_all", [P, EXPERTS], BF16)
        slot = sb("slot", [P, QUAD, EXPERTS])
        slot_k = sb("slot_k", [P, QUAD, TOP_K, EXPERTS])
        ROWS = sb("ROWS", [P, 2, QUAD, TOP_K], U32)
        gate_e = sb("gate_e", [P, QUAD, TOP_K])
        gate_1 = sb("gate_1", [P, QUAD, TOP_K])
        pad = sb("pad", [P, ROW])
        pad_at = sb("pad_at", [1, EXPERTS], I32)
        nb_a = sb("nb_a", [EXPERTS, P], I32)
        nb_b = sb("nb_b", [EXPERTS, P], I32)
        nb = sb("nb", [EXPERTS, P])
        before = sb("before", [P, EXPERTS])
        before_nb = sb("before_nb", [P, EXPERTS])
        blk = sb("blk", [P, 8])
        table_f = sb("table_f", [P, 2])
        table = sb("table", [1, 2, P], I32)
        XS = sb("XS", [P, BODY, ROW])
        Y = sb("Y", [P, BODY, D])
        xT = sb("xT", [P, 2, P])
        sg = sb("sg", [P, 2, EXP_DIM])
        h = sb("h", [P, 2, EXP_DIM])
        hT = sb("hT", [P, 2, P])
        sh_s = sb("sh_s", [P, 2, 2 * HALF])
        sh_h = sb("sh_h", [P, 2, 2 * HALF])
        YL = sb("YL", [P, 2, TOP_K, QTOK])
        ysum = sb("ysum", [P, 2, QTOK])

        pT = pb("pT", [P, 512])
        pQ = pb("pQ", [P, 512])
        pKVN = pb("pKVN", [P, QUAD, 256])
        pKV = pb("pKV", [P, 2, 256])
        pN = pb("pN", [P, QUAD, 256])
        pZ = pb("pZ", [P, 512])
        pO = pN[:, 0:2, :].rearrange("p a c -> p (a c)")
        pL = pZ[:, 0:QUAD * EXPERTS].rearrange("p (t e) -> p t e", e=EXPERTS)
        pR = pZ[:, 128:128 + QUAD * EXPERTS].rearrange("p (t e) -> p t e", e=EXPERTS)
        pX = pT[:, 0:P]
        pGU = [pQ, pZ]
        pHT = pKV[:, 0, 0:P]
        pY = pKVN[:, 0, 0:D]
        pSG = pKVN[:, 2:4, :].rearrange("p a c -> p (a c)")
        pSU = pN[:, 0:2, :].rearrange("p a c -> p (a c)")
        pSD = pN[:, 2, :]

        s_cn, s_wa, s_wf = sem("s_cn"), sem("s_wa"), sem("s_wf")
        waited = sem("waited")
        s_x = sem("s_x")
        s_ones, s_tri, s_bo, s_bo_all = sem("s_ones"), sem("s_tri"), sem("s_bo"), sem("s_bo_all")
        s_xb = sem("s_xb")
        a_stats, a_aggr, a_rstd, a_norm = sem("a_stats"), sem("a_aggr"), sem("a_rstd"), sem("a_norm")
        a_ln, a_y, a_n1, a_n2 = sem("a_ln"), sem("a_y"), sem("a_n1"), sem("a_n2")
        c_ln, c_y, c_n1, c_n2 = sem("c_ln"), sem("c_y"), sem("c_n1"), sem("c_n2")
        a_T, a_xT, a_q, a_kv = sem("a_T"), sem("a_xT"), sem("a_q"), sem("a_kv")
        a_rk, a_ek, a_rq, a_eq, a_v = sem("a_rk"), sem("a_ek"), sem("a_rq"), sem("a_eq"), sem("a_v")
        a_kf, a_qf = sem("a_kf"), sem("a_qf")
        b_kv, b_mask1, b_mask, b_num = sem("b_kv"), sem("b_mask1"), sem("b_mask"), sem("b_num")
        b_den, b_rden, b_att = sem("b_den"), sem("b_rden"), sem("b_att")
        b_T, b_aT, b_wo = sem("b_T"), sem("b_aT"), sem("b_wo")
        c_x1, c_stats, c_aggr, c_rstd = sem("c_x1"), sem("c_stats"), sem("c_aggr"), sem("c_rstd")
        c_z, c_zdup, c_T, c_zT, c_zT2 = sem("c_z"), sem("c_zdup"), sem("c_T"), sem("c_zT"), sem("c_zT2")
        c_lg, c_lgs, c_top, c_idx, c_idf = sem("c_lg"), sem("c_lgs"), sem("c_top"), sem("c_idx"), sem("c_idf")
        c_oh, c_ch, c_rank, c_chq, c_cha = sem("c_oh"), sem("c_ch"), sem("c_rank"), sem("c_chq"), sem("c_cha")
        c_slot, c_slotk, c_rows = sem("c_slot"), sem("c_slotk"), sem("c_rows")
        c_ge, c_g1, c_pay = sem("c_ge"), sem("c_g1"), sem("c_pay")
        scat = [sem("scat0"), sem("scat1")]
        t_cnt, t_nba, t_nbb, t_nb, t_cum = sem("t_cnt"), sem("t_nba"), sem("t_nbb"), sem("t_nb"), sem("t_cum")
        t_v, t_tab, t_row, t_table, t_pad, t_pads = (sem("t_v"), sem("t_tab"), sem("t_row"),
                                                     sem("t_table"), sem("t_pad"), sem("t_pads"))
        xs = [sem(f"xs{j}") for j in range(BODY)]
        ysc = [sem(f"ysc{j}") for j in range(BODY)]
        s_Tx, s_xT, s_gu, s_silu, s_h = sem("s_Tx"), sem("s_xT"), sem("s_gu"), sem("s_silu"), sem("s_h")
        s_Th, s_hT, s_D, s_y = sem("s_Th"), sem("s_hT"), sem("s_D"), sem("s_y")
        h_gu, h_silu, h_h, h_d, h_add = sem("h_gu"), sem("h_silu"), sem("h_h"), sem("h_d"), sem("h_add")
        yl = [sem("yl0"), sem("yl1")]
        c_sum, c_out, s_out = sem("c_sum"), sem("c_out"), sem("s_out")

        def wait(eng, semaphore, count):
            if not isinstance(count, int) or count > 0:
                eng.wait_ge(semaphore, count)

        def quad(t, q):
            return t[:, bass.ds(q * QTOK, QTOK)]

        def steps(eng, step):
            for s in range(3):
                step(s, s % 2)
            with eng.Fori(0, 2) as it:
                for u in range(2):
                    step(it * 2 + (3 + u), (3 + u) % 2)
            for s in range(7, NQ + 2):
                step(s, s % 2)

        def wait_apart(eng, semaphore, count):
            eng.wait_ge(semaphore, count)
            eng.sem_inc(waited, 1)

        def has(s, lag):
            return not isinstance(s, int) or 0 <= s - lag < NQ

        block = ctx.enter_context(nc.Block())

        @block.sync
        def _(sp):
            sp.dma_start(quad(X, 0).rearrange("p (b f) -> p b f", b=SPQ), x_v[0]).then_inc(s_x, 16)
            sp.dma_start(bo_row[0:1, :], bo).then_inc(s_bo, 16)
            sp.wait_ge(s_x, 16)
            with sp.Fori(1, NQ) as q:
                sp.dma_start(quad(X, q).rearrange("p (b f) -> p b f", b=SPQ),
                             x_v[bass.ds(q, 1)].rearrange("o p b f -> (o p) b f")).then_inc(s_x, 16)
                wait_apart(sp, s_x, q * 16 + 16)

            sp.wait_ge(t_pad, 2)
            with sp.Fori(0, EXPERTS) as e:
                at = sp.value_load(pad_at[0:1, bass.ds(e, 1)], min_val=0, max_val=EXPERTS * REGION - P)
                sp.dma_start(routed[bass.ds(at, P), :], pad[:, :]).then_inc(t_pads, 16)
            sp.dma_start(routed[EXPERTS * REGION:EXPERTS * REGION + P, :], pad[:, :]).then_inc(t_pads, 16)
            sp.wait_ge(t_pads, 16 * (EXPERTS + 1))
            for s_ in scat:
                sp.wait_ge(s_, 16 * QUAD * TOP_K * NQ // 2)
            sp.wait_ge(t_table, 1)

            def load(it, j):
                b = sp.value_load(table[0:1, 0, bass.ds(it * BODY + j, 1)], min_val=0,
                                  max_val=EXPERTS * REGION_BLOCKS)
                wait(sp, ysc[j], it * 16)
                sp.dma_start(XS[:, j, :], routed[bass.ds(b * P, P), :]).then_inc(xs[j], 16)

            for j in range(BODY):
                load(0, j)
            with sp.Fori(1, TURNS) as it:
                for j in range(BODY):
                    load(it, j)

            for s_ in ysc:
                sp.wait_ge(s_, 16 * TURNS)

            def load_y(q, par):
                for k in range(TOP_K):
                    sp.dma_start(YL[:, par, k, :].rearrange("p (b f) -> p b f", b=SPQ),
                                 res_v[k, bass.ds(q, 1)].rearrange("o p b f -> (o p) b f")
                                 ).then_inc(yl[par], 16)

            for q in range(2):
                load_y(q, q)
            with sp.Fori(1, NQ // 2) as it:
                for par in range(2):
                    sp.wait_ge(c_sum, it * 2 + (par - 1))
                    load_y(it * 2 + par, par)
            sp.wait_ge(s_out, 16 * NQ)

        @block.gpsimd
        def _(pool):
            pool.wait_ge(s_bo_all, 2)
            bo_q = bo_all[:, :].unsqueeze(1).to_broadcast([P, QUAD, D])
            with pool.Fori(0, NQ) as q:
                pool.wait_ge(s_x, q * 16 + 16)
                nc.gpsimd.tensor_tensor(quad(X1, q).rearrange("p (t c) -> p t c", t=QUAD),
                                        quad(X, q).rearrange("p (t c) -> p t c", t=QUAD),
                                        bo_q, ALU.add).then_inc(s_xb, 1)

            def dispatch(q, par):
                pool.wait_ge(c_rows, q + 1)
                pool.wait_ge(c_pay, q + 1)
                wait_apart(pool, c_zdup, q + 1)
                for t in range(QUAD):
                    for k in range(TOP_K):
                        nc.gpsimd.indirect_dma_start(
                            routed, bass.IndirectOffsetOnAxis(ap=ROWS[:, par, t, k:k + 1], axis=0),
                            Z[:, par, t, k, :], None).then_inc(scat[par], 16)

            with pool.Fori(0, NQ // 2) as it:
                for par in range(2):
                    dispatch(it * 2 + par, par)

            with pool.Fori(0, TURNS) as it:
                for j in range(BODY):
                    wait_apart(pool, s_y, it * BODY + (j + 1))
                    nc.gpsimd.indirect_dma_start(
                        results, bass.IndirectOffsetOnAxis(ap=XS[:, j, D:D + 1].bitcast(U32), axis=0),
                        Y[:, j, :], None, bounds_check=PAIRS - 1, oob_is_err=False).then_inc(ysc[j], 16)

            with pool.Fori(0, NQ // 2) as it:
                for par in range(2):
                    pool.wait_ge(yl[par], it * 32 + 32)
                    nc.gpsimd.tensor_tensor(ysum[:, par, :], YL[:, par, 0, :], YL[:, par, 1, :],
                                            ALU.add).then_inc(c_sum, 1)
                    pool.wait_ge(c_out, it * 2 + (par + 1))

        @block.scalar
        def _(act):
            act.dma_start(CN[:, :], consts).then_inc(s_cn, 16)
            act.dma_start(WA[:, :], w_att).then_inc(s_wa, 16)
            act.dma_start(TOK[:, :], tokid).then_inc(s_cn, 16)
            act.dma_start(WF[:, :], w_ffn).then_inc(s_wf, 16)

            def rstd(mv, rs, aggr, ln, y, q):
                act.wait_ge(aggr, q + 1)
                nc.scalar.activation(rs[:, 0, :], mv[:, :, 1], ACT.Ln, bias=eps[:, 0:1]).then_inc(ln, 1)
                act.wait_ge(ln, q + 1)
                nc.scalar.activation(rs[:, 1, :], rs[:, 0, :], ACT.Exp, scale=-0.5).then_inc(y, 1)

            act.wait_ge(s_tri, 1)
            rstd(a_mv, a_rs, a_aggr, a_ln, a_y, 0)

            def step(s, par):
                par1, par2 = 1 - par, par
                if has(s, 0):
                    act.wait_ge(a_T, s + 1)
                    wait(act, a_kv, s - 1)
                    nc.scalar.copy(XNT[:, par, :], pT[:, :]).then_inc(a_xT, 1)
                if has(s, 2):
                    q = s - 2
                    rstd(c_mv, c_rs, c_aggr, c_ln, c_y, q)
                    act.wait_ge(c_z, q + 1)
                    nc.scalar.copy(Z[:, par2, :, 1, 0:D], Z[:, par2, :, 0, 0:D]).then_inc(c_zdup, 1)
                if has(s, 0):
                    act.wait_ge(a_q, s + 1)
                    nc.scalar.activation(rq[:, :], pQ[:, :], ACT.Relu, scale=-1.0).then_inc(a_rq, 1)
                    act.wait_ge(a_rq, s + 1)
                    wait(act, a_qf, s)
                    nc.scalar.activation(eq[:, :], rq[:, :], ACT.Exp, scale=-1.0).then_inc(a_eq, 1)
                    act.wait_ge(a_kv, s + 1)
                    nc.scalar.activation(rk[:, :, :], pKVN[:, :, 0:D], ACT.Relu, scale=-1.0).then_inc(a_rk, 1)
                    wait(act, b_kv, s - 1)
                    nc.scalar.copy(V[:, par, :, 0:D], pKVN[:, :, D:2 * D]).then_inc(a_v, 1)
                    act.wait_ge(a_rk, s + 1)
                    wait(act, a_kf, s)
                    nc.scalar.activation(ek[:, :, :], rk[:, :, :], ACT.Exp, scale=-1.0).then_inc(a_ek, 1)
                if has(s, 2):
                    q = s - 2
                    act.wait_ge(c_T, q + 1)
                    wait(act, c_lg, q)
                    nc.scalar.copy(zT[:, :], pZ[:, :]).then_inc(c_zT, 1)
                    act.wait_ge(c_zT, q + 1)
                    nc.scalar.copy(quad(ZT, q), zT[:, :]).then_inc(c_zT2, 1)
                if has(s, 1):
                    q = s - 1
                    act.wait_ge(b_T, q + 1)
                    wait(act, b_wo, q)
                    nc.scalar.copy(attT[:, :], pT[:, :]).then_inc(b_aT, 1)
                if not isinstance(s, int) or s + 1 < NQ:
                    rstd(a_mv, a_rs, a_aggr, a_ln, a_y, s + 1)
                if has(s, 2):
                    q = s - 2
                    act.wait_ge(c_top, q + 1)
                    wait(act, c_g1, q)
                    nc.scalar.activation(gate_e[:, :, :], top[:, :, 0:TOP_K], ACT.Exp, scale=-1.0).then_inc(c_ge, 1)

            steps(act, step)

            def silu(n, j):
                act.wait_ge(s_gu, n + 1)
                wait(act, s_h, n - 1)
                nc.scalar.activation(sg[:, j % 2, :], pGU[j % 2][:, 0:EXP_DIM], ACT.Silu).then_inc(s_silu, 1)

            def scaled(n, j):
                act.wait_ge(s_D, n + 1)
                nc.scalar.activation(Y[:, j, :], pY, ACT.Copy, scale=XS[:, j, D + 1:D + 2]).then_inc(s_y, 1)

            def shared(i, par):
                act.wait_ge(h_gu, i + 1)
                wait(act, h_h, i - 1)
                nc.scalar.activation(sh_s[:, par, :], pSG, ACT.Silu).then_inc(h_silu, 1)

            def body(it, first):
                for j in range(BODY):
                    n = it * BODY + j
                    if j % 5 == 1:
                        shared(it * 2 + j // 5, j // 5)
                    if not (first and j < 1):
                        silu(n - 1, (j - 1) % BODY)
                    if not (first and j < 3):
                        scaled(n - 3, (j - 3) % BODY)

            body(0, True)
            with act.Fori(1, TURNS) as it:
                body(it, False)
            silu(BLOCKS - 1, BODY - 1)
            for k in range(3):
                scaled(BLOCKS - 3 + k, BODY - 3 + k)

            with act.Fori(0, NQ) as q:
                act.wait_ge(c_out, q + 1)
                act.dma_start(out_v[bass.ds(q, 1)].rearrange("o p b f -> (o p) b f"),
                              quad(X1, q).rearrange("p (b f) -> p b f", b=SPQ)).then_inc(s_out, 16)

        @block.vector
        def _(dve):
            nc.vector.memset(ones_row[:, :], 1.0)
            nc.vector.memset(ones[:, :], 1.0)
            nc.vector.memset(chosen_all[:, :], 0.0)
            nc.vector.memset(eps[:, :], LN_EPS)
            nc.vector.memset(pad[:, :], 0.0).then_inc(t_pad, 1)
            nc.vector.memset(V[:, :, :, D:D + 1], 1.0).then_inc(s_ones, 1)
            dve.wait_ge(t_pad, 1)
            nc.vector.memset(pad[:, D:D + 1].bitcast(U32), SKIP).then_inc(s_ones, 1)
            dve.wait_ge(s_cn, 32)
            nc.vector.tensor_copy(tri[:, :], CN[:, C_TRI:C_TRI + P]).then_inc(s_tri, 1)
            dve.wait_ge(s_bo_all, 1)
            nc.vector.tensor_copy(bo_all[:, :], pQ[:, 0:D]).then_inc(s_bo_all, 1)

            def norm_stats(src, stat, mv, stats, aggr, q):
                for t in range(QUAD):
                    i = nc.vector.bn_stats(stat[:, t, :], src[:, bass.ds(q * QTOK + t * D, D)])
                i.then_inc(stats, 1)
                wait_apart(dve, stats, q + 1)
                for t in range(QUAD):
                    i = nc.vector.bn_aggr(mv[:, t, :], stat[:, t, :])
                i.then_inc(aggr, 1)

            def newton(mv, rs, y, n1, n2, rstd, q):
                dve.wait_ge(y, q + 1)
                nc.vector.scalar_tensor_tensor(rs[:, 2, :], mv[:, :, 1], LN_EPS, rs[:, 1, :], ALU.add, ALU.mult).then_inc(n1, 1)
                dve.wait_ge(n1, q + 1)
                nc.vector.scalar_tensor_tensor(rs[:, 3, :], rs[:, 2, :], -0.5, rs[:, 1, :], ALU.mult, ALU.mult).then_inc(n2, 1)
                dve.wait_ge(n2, q + 1)
                nc.vector.scalar_tensor_tensor(rs[:, 4, :], rs[:, 3, :], 1.5, rs[:, 1, :], ALU.add, ALU.mult).then_inc(rstd, 1)
                dve.wait_ge(rstd, q + 1)

            def stats1(q):
                wait_apart(dve, s_x, q * 16 + 16)
                norm_stats(X, a_stat, a_mv, a_stats, a_aggr, q)

            def norm1(q, par):
                newton(a_mv, a_rs, a_y, a_n1, a_n2, a_rstd, q)
                wait(dve, a_T, q - 1)
                for t in range(QUAD):
                    i = nc.vector.tensor_scalar(XN[:, par, t, :], X[:, bass.ds(q * QTOK + t * D, D)],
                                                a_mv[:, t, 0:1], a_rs[:, 4, t:t + 1], ALU.subtract, ALU.mult)
                i.then_inc(a_norm, 1)

            def residual(q):
                dve.wait_ge(b_wo, q + 1)
                dve.wait_ge(s_xb, q + 1)
                nc.vector.tensor_tensor(quad(X1, q), pO, quad(X1, q), ALU.add).then_inc(c_x1, 1)
                wait_apart(dve, c_x1, q + 1)
                norm_stats(X1, c_stat, c_mv, c_stats, c_aggr, q)

            def norm2(q, par, turn):
                newton(c_mv, c_rs, c_y, c_n1, c_n2, c_rstd, q)
                wait(dve, scat[par], turn)
                for t in range(QUAD):
                    i = nc.vector.tensor_scalar(Z[:, par, t, 0, 0:D], X1[:, bass.ds(q * QTOK + t * D, D)],
                                                c_mv[:, t, 0:1], c_rs[:, 4, t:t + 1], ALU.subtract, ALU.mult)
                i.then_inc(c_z, 1)

            def mask(q):
                dve.wait_ge(b_kv, q + 1)
                wait(dve, b_num, q)
                nc.vector.tensor_tensor(
                    KV[:, :, 0:D], pKV[:, :, 0:D],
                    CN[:, C_MASK:C_MASK + D].unsqueeze(1).to_broadcast([P, SPQ, D]), ALU.mult).then_inc(b_mask1, 1)
                nc.vector.tensor_tensor(
                    KV[:, :, D:RK], pKV[:, :, D:D + 1].to_broadcast([P, SPQ, HEADS]),
                    CN[:, C_MASK + D:C_MASK + RK].unsqueeze(1).to_broadcast([P, SPQ, HEADS]),
                    ALU.mult).then_inc(b_mask, 1)

            def attend(q):
                dve.wait_ge(b_num, q + 1)
                nc.vector.tensor_scalar(den[:, :, :], pN[:, :, D:RK], ATT_EPS, None, ALU.add).then_inc(b_den, 1)
                dve.wait_ge(b_den, q + 1)
                nc.vector.reciprocal(rden[:, :, :], den[:, :, :]).then_inc(b_rden, 1)
                dve.wait_ge(b_rden, q + 1)
                wait(dve, b_T, q)
                nc.vector.tensor_tensor(
                    att[:, :, :].rearrange("p t (h d) -> p t h d", d=HD),
                    pN[:, :, 0:D].rearrange("p t (h d) -> p t h d", d=HD),
                    rden[:, :, :].unsqueeze(3).to_broadcast([P, QUAD, HEADS, HD]), ALU.mult).then_inc(b_att, 1)

            def features(q, par):
                dve.wait_ge(a_eq, q + 1)
                wait(dve, b_num, q - 1)
                nc.vector.scalar_tensor_tensor(QF[:, par, :], pQ[:, :], 1.0, eq[:, :], ALU.add, ALU.max).then_inc(a_qf, 1)
                dve.wait_ge(a_ek, q + 1)
                wait(dve, b_kv, q - 1)
                nc.vector.scalar_tensor_tensor(KF[:, par, :, :], pKVN[:, :, 0:D], 1.0, ek[:, :, :],
                                               ALU.add, ALU.max).then_inc(a_kf, 1)

            def route(q, par):
                dve.wait_ge(c_lg, q + 1)
                nc.vector.tensor_copy(logits[:, :, :], pL).then_inc(c_lgs, 1)
                wait_apart(dve, c_lgs, q + 1)
                for t in range(QUAD):
                    i = nc.vector.max(top[:, t, :], logits[:, t, :])
                i.then_inc(c_top, 1)
                wait_apart(dve, c_top, q + 1)
                for t in range(QUAD):
                    i = nc.vector.max_index(top_i[:, t, :], top[:, t, :], logits[:, t, :])
                i.then_inc(c_idx, 1)
                dve.wait_ge(c_idx, q + 1)
                nc.vector.tensor_copy(top_f[:, :, :], top_i[:, :, 0:TOP_K]).then_inc(c_idf, 1)
                dve.wait_ge(c_idf, q + 1)
                nc.vector.tensor_tensor(
                    onehot[:, :, :, :].rearrange("p t k e -> p (t k) e"),
                    CN[:, C_IOTA:C_IOTA + EXPERTS].unsqueeze(1).to_broadcast([P, QUAD * TOP_K, EXPERTS]),
                    top_f[:, :, :].rearrange("p t k -> p (t k)").unsqueeze(2).to_broadcast([P, QUAD * TOP_K, EXPERTS]),
                    ALU.is_equal).then_inc(c_oh, 1)
                dve.wait_ge(c_oh, q + 1)
                nc.vector.tensor_tensor(chosen[:, :, :], onehot[:, :, 0, :], onehot[:, :, 1, :], ALU.add).then_inc(c_ch, 1)
                dve.wait_ge(c_ge, q + 1)
                nc.vector.tensor_scalar(gate_1[:, :, :], gate_e[:, :, :], 1.0, None, ALU.add).then_inc(c_g1, 1)
                nc.vector.tensor_copy(Z[:, par, :, :, D].bitcast(U32),
                                      TOK[:, bass.ds(q * QUAD * TOP_K, QUAD * TOP_K)].rearrange("p (t k) -> p t k", k=TOP_K))
                dve.wait_ge(c_g1, q + 1)
                nc.vector.reciprocal(Z[:, par, :, :, D + 1], gate_1[:, :, :]).then_inc(c_pay, 1)
                with nc.allow_low_precision("counts up to 32 are exact in bfloat16"):
                    nc.vector.tensor_reduce(chosen_q[:, :], chosen[:, :, :].rearrange("p t e -> p e t"), AX.X, ALU.add).then_inc(c_chq, 1)
                dve.wait_ge(c_rank, q + 1)
                nc.vector.tensor_tensor(
                    slot[:, :, :], pR,
                    CN[:, C_BASE:C_BASE + EXPERTS].unsqueeze(1).to_broadcast([P, QUAD, EXPERTS]), ALU.add).then_inc(c_slot, 1)
                dve.wait_ge(c_chq, q + 1)
                nc.vector.tensor_tensor(chosen_all[:, :], chosen_all[:, :], chosen_q[:, :], ALU.add).then_inc(c_cha, 1)
                dve.wait_ge(c_slot, q + 1)
                nc.vector.tensor_tensor(slot_k[:, :, :, :], onehot[:, :, :, :],
                                        slot[:, :, :].unsqueeze(2).to_broadcast([P, QUAD, TOP_K, EXPERTS]),
                                        ALU.mult).then_inc(c_slotk, 1)
                dve.wait_ge(c_slotk, q + 1)
                with nc.allow_low_precision("row numbers are whole and below 2 ** 24"):
                    nc.vector.tensor_reduce(ROWS[:, par, :, :], slot_k[:, :, :, :], AX.X, ALU.add).then_inc(c_rows, 1)

            def step(s, par):
                par1 = 1 - par
                if has(s, 2):
                    residual(s - 2)
                if has(s, 1):
                    mask(s - 1)
                if has(s, 2):
                    q = s - 2
                    turn = (q // 2) * 128 if isinstance(q, int) else dve_turn(s, par)
                    norm2(q, par, turn)
                if has(s, 1):
                    attend(s - 1)
                if has(s, 0):
                    features(s, par)
                if not isinstance(s, int) or s + 1 < NQ:
                    stats1(s + 1)
                if has(s, 2):
                    route(s - 2, par)
                if not isinstance(s, int) or s + 1 < NQ:
                    norm1(s + 1, par1)

            def dve_turn(s, par):
                q = s - 2
                return (q - 1) * 64 if par == 1 else q * 64

            stats1(0)
            norm1(0, 0)
            dve.wait_ge(s_tri, 1)
            steps(dve, step)

            dve.wait_ge(t_cnt, 1)
            cnt = pZ[0:EXPERTS, 0:P]
            nc.vector.tensor_scalar(nb_a[:, :], cnt, float(P - 1), None, ALU.add).then_inc(t_nba, 1)
            nc.vector.tensor_tensor(pad_at[0:1, :], pZ[0:1, 256:256 + EXPERTS], CN[0:1, C_BASE:C_BASE + EXPERTS],
                                    ALU.add).then_inc(t_pad, 1)
            dve.wait_ge(t_nba, 1)
            nc.vector.tensor_single_scalar(nb_b[:, :], nb_a[:, :], 7, ALU.arith_shift_right).then_inc(t_nbb, 1)
            dve.wait_ge(t_nbb, 1)
            nc.vector.tensor_copy(nb[:, :], nb_b[:, :]).then_inc(t_nb, 1)
            dve.wait_ge(t_cum, 1)
            cum = pZ[:, 0:EXPERTS]
            nbs = pZ[:, EXPERTS:2 * EXPERTS]
            slot_id = CN[:, C_SLOT:C_SLOT + 1]
            nc.vector.tensor_scalar(before[:, :], cum, slot_id, None, ALU.is_le).then_inc(t_v, 1)
            dve.wait_ge(t_v, 1)
            nc.vector.tensor_tensor(before_nb[:, :], before[:, :], nbs, ALU.mult).then_inc(t_v, 1)
            nc.vector.tensor_reduce(blk[:, 0:1], before[:, :], AX.X, ALU.add).then_inc(t_v, 1)
            dve.wait_ge(t_v, 3)
            nc.vector.tensor_reduce(blk[:, 1:2], before_nb[:, :], AX.X, ALU.add).then_inc(t_v, 1)
            nc.vector.tensor_scalar(blk[:, 2:3], blk[:, 0:1], float(REGION_BLOCKS), slot_id, ALU.mult, ALU.add).then_inc(t_v, 1)
            nc.vector.tensor_scalar(table_f[:, 1:2], blk[:, 0:1], float(EXPERTS - 1), None, ALU.min)
            dve.wait_ge(t_v, 5)
            nc.vector.tensor_scalar(table_f[:, 0:1], blk[:, 2:3], blk[:, 1:2], float(EXPERTS * REGION_BLOCKS),
                                    ALU.subtract, ALU.min).then_inc(t_tab, 1)
            dve.wait_ge(t_row, 1)
            nc.vector.tensor_copy(table[0:1, :, :], pZ[0:1, 128:128 + 2 * P].rearrange("p (a b) -> p a b", a=2)).then_inc(t_table, 1)

            def rows(n, j):
                dve.wait_ge(s_Tx, n + 1)
                wait(dve, s_gu, n - 1)
                nc.vector.tensor_copy(xT[:, j % 2, :], pX).then_inc(s_xT, 1)

            def hidden(n, j):
                dve.wait_ge(s_silu, n + 1)
                wait(dve, s_Th, n - 1)
                nc.vector.tensor_tensor(h[:, j % 2, :], pGU[j % 2][:, EXP_DIM:2 * EXP_DIM], sg[:, j % 2, :],
                                        ALU.mult).then_inc(s_h, 1)

            def hidden_t(n, j):
                dve.wait_ge(s_Th, n + 1)
                wait(dve, s_D, n - 1)
                nc.vector.tensor_copy(hT[:, j % 2, :], pHT).then_inc(s_hT, 1)

            def shared_h(i, par):
                dve.wait_ge(h_silu, i + 1)
                wait(dve, h_d, i - 1)
                nc.vector.tensor_tensor(sh_h[:, par, :], pSU, sh_s[:, par, :], ALU.mult).then_inc(h_h, 1)

            def shared_add(i):
                dve.wait_ge(h_d, i + 1)
                x1 = X1[:, bass.ds(i * HALF, HALF)]
                nc.vector.tensor_tensor(x1, pSD, x1, ALU.add).then_inc(h_add, 1)

            def body(it, first):
                for j in range(BODY):
                    n = it * BODY + j
                    if j % 5 == 1:
                        shared_h(it * 2 + j // 5, j // 5)
                    if j % 5 == 3:
                        shared_add(it * 2 + j // 5)
                    rows(n, j)
                    if not (first and j < 1):
                        hidden(n - 1, (j - 1) % BODY)
                    if not (first and j < 2):
                        hidden_t(n - 2, (j - 2) % BODY)

            body(0, True)
            with dve.Fori(1, TURNS) as it:
                body(it, False)
            hidden(BLOCKS - 1, BODY - 1)
            hidden_t(BLOCKS - 2, BODY - 2)
            hidden_t(BLOCKS - 1, BODY - 1)

            dve.wait_ge(h_add, HALVES)
            with dve.Fori(0, NQ // 2) as it:
                for par in range(2):
                    q = it * 2 + par
                    dve.wait_ge(c_sum, q + 1)
                    nc.vector.tensor_tensor(quad(X1, q), quad(X1, q), ysum[:, par, :], ALU.add).then_inc(c_out, 1)

        @block.tensor
        def _(pe):
            pe.wait_ge(s_ones, 2)
            pe.wait_ge(s_bo, 16)
            pe.wait_ge(s_cn, 32)
            pe.wait_ge(s_wa, 16)

            def step(s, par):
                par1 = 1 - par
                if has(s, 0):
                    pe.wait_ge(a_norm, s + 1)
                    wait(pe, b_aT, s - 1)
                    wait(pe, a_xT, s)
                    for t in range(QUAD):
                        i = nc.tensor.transpose(pT[:, t * P:(t + 1) * P], XN[:, par, t, :], ident)
                    i.then_inc(a_T, 1)
                if has(s, 1):
                    q = s - 1
                    pe.wait_ge(a_kf, q + 1)
                    pe.wait_ge(a_v, q + 1)
                    wait(pe, b_mask, q)
                    for b in range(SPQ):
                        for j in range(2):
                            i = nc.tensor.matmul(pKV[:, b, 0:D + 1], KF[:, par1, 2 * b + j, :],
                                                 V[:, par1, 2 * b + j, 0:D + 1], start=(j == 0), stop=(j == 1))
                    i.then_inc(b_kv, 1)
                if has(s, 0):
                    pe.wait_ge(a_xT, s + 1)
                    wait(pe, a_qf, s)
                    nc.tensor.matmul(pQ[:, :], WA[:, W_Q:W_Q + D], XNT[:, par, :], start=True, stop=True).then_inc(a_q, 1)
                if has(s, 1):
                    q = s - 1
                    pe.wait_ge(a_qf, q + 1)
                    pe.wait_ge(b_mask, q + 1)
                    wait(pe, b_att, q)
                    wait(pe, c_x1, q)
                    for t in range(QUAD):
                        i = nc.tensor.matmul(pN[:, t, 0:RK], QF[:, par1, t * P:(t + 1) * P], KV[:, t // 2, :],
                                             start=True, stop=True)
                    i.then_inc(b_num, 1)
                if has(s, 0):
                    wait(pe, a_kf, s)
                    wait(pe, a_v, s)
                    for t in range(QUAD):
                        i = nc.tensor.matmul(pKVN[:, t, :], XNT[:, par, t * P:(t + 1) * P], WA[:, W_KV:W_KV + 2 * D],
                                             start=True, stop=True)
                    i.then_inc(a_kv, 1)
                if has(s, 2):
                    q = s - 2
                    pe.wait_ge(c_z, q + 1)
                    wait(pe, c_slot, q)
                    for t in range(QUAD):
                        i = nc.tensor.transpose(pZ[:, t * P:(t + 1) * P], Z[:, par, t, 0, 0:D], ident)
                    i.then_inc(c_T, 1)
                if has(s, 1):
                    q = s - 1
                    pe.wait_ge(b_att, q + 1)
                    for t in range(QUAD):
                        i = nc.tensor.transpose(pT[:, t * P:(t + 1) * P], att[:, t, :], ident)
                    i.then_inc(b_T, 1)
                if has(s, 2):
                    q = s - 2
                    pe.wait_ge(c_zT, q + 1)
                    for t in range(QUAD):
                        i = nc.tensor.matmul(pL[:, t, :], zT[:, t * P:(t + 1) * P], WA[:, W_R:W_R + EXPERTS],
                                             start=True, stop=True)
                    i.then_inc(c_lg, 1)
                if has(s, 1):
                    q = s - 1
                    pe.wait_ge(b_aT, q + 1)
                    for t in range(QUAD):
                        i = nc.tensor.matmul(pO[:, t * P:(t + 1) * P], attT[:, t * P:(t + 1) * P], WA[:, W_O:W_O + D],
                                             start=True, stop=True)
                    i.then_inc(b_wo, 1)
                if has(s, 2):
                    q = s - 2
                    pe.wait_ge(c_ch, q + 1)
                    wait(pe, c_cha, q)
                    nc.tensor.matmul(pR, tri[:, :], chosen[:, :, :], start=True, stop=False)
                    for t in range(QUAD - 1):
                        nc.tensor.matmul(pR[:, t + 1:QUAD, :], ones[:, :],
                                         chosen[:, t:t + 1, :].to_broadcast([P, QUAD - 1 - t, EXPERTS]),
                                         start=False, stop=False)
                    nc.tensor.matmul(pR, ones[:, :], chosen_all[:, :].unsqueeze(1).to_broadcast([P, QUAD, EXPERTS]),
                                     start=False, stop=True).then_inc(c_rank, 1)

            nc.tensor.matmul(pQ[:, 0:D], ones_row[0:1, :], bo_row[0:1, :], start=True, stop=True).then_inc(s_bo_all, 1)
            pe.wait_ge(s_tri, 1)
            pe.wait_ge(s_bo_all, 2)
            steps(pe, step)

            pe.wait_ge(c_cha, NQ)
            pe.wait_ge(c_slot, NQ)
            nc.tensor.matmul(pZ[0:EXPERTS, 0:P], chosen_all[:, :], ones[:, :], start=True, stop=True)
            nc.tensor.matmul(pZ[0:1, 256:256 + EXPERTS], ones[:, 0:1], chosen_all[:, :], start=True, stop=True).then_inc(t_cnt, 1)
            pe.wait_ge(t_nb, 1)
            pe.wait_ge(t_pad, 2)
            nc.tensor.matmul(pZ[:, 0:2 * EXPERTS], nb[:, :], CN[0:EXPERTS, C_CUM:C_CUM + 2 * EXPERTS],
                             start=True, stop=True).then_inc(t_cum, 1)
            pe.wait_ge(t_tab, 1)
            for a in range(2):
                i = nc.tensor.matmul(pZ[0:1, 128 + a * P:128 + (a + 1) * P], table_f[:, a:a + 1], ident, start=True, stop=True)
            i.then_inc(t_row, 1)

            def rows_t(n, it, j):
                pe.wait_ge(xs[j], it * 16 + 16)
                wait(pe, s_xT, n)
                nc.tensor.transpose(pX, XS[:, j, 0:D], ident).then_inc(s_Tx, 1)

            def expert(n):
                return pe.value_load(table[0:1, 1, bass.ds(n, 1)], min_val=0, max_val=EXPERTS - 1)

            def gate_up(n, j):
                e = expert(n)
                pe.wait_ge(s_xT, n + 1)
                wait(pe, s_h, n - 1)
                nc.tensor.matmul(pGU[j % 2][:, 0:2 * EXP_DIM], xT[:, j % 2, :],
                                 WF[:, bass.ds(e * (2 * EXP_DIM) + F_GU, 2 * EXP_DIM)], start=True, stop=True).then_inc(s_gu, 1)

            def hidden_t(n, j):
                pe.wait_ge(s_h, n + 1)
                wait(pe, s_hT, n)
                nc.tensor.transpose(pHT, h[:, j % 2, :], ident).then_inc(s_Th, 1)

            def down(n, j):
                e = expert(n)
                pe.wait_ge(s_hT, n + 1)
                wait(pe, s_y, n)
                nc.tensor.matmul(pY, hT[:, j % 2, :], WF[:, bass.ds(e * D + F_DN, D)], start=True, stop=True).then_inc(s_D, 1)

            def shared_gu(i):
                wait(pe, h_h, i)
                zt = ZT[:, bass.ds(i * HALF, HALF)]
                for f in range(2):
                    nc.tensor.matmul(pSG[:, f * HALF:(f + 1) * HALF], WF[:, F_SG + f * P:F_SG + (f + 1) * P], zt, start=True, stop=True)
                    l = nc.tensor.matmul(pSU[:, f * HALF:(f + 1) * HALF], WF[:, F_SU + f * P:F_SU + (f + 1) * P], zt, start=True, stop=True)
                l.then_inc(h_gu, 1)

            def shared_d(i, par):
                pe.wait_ge(h_h, i + 1)
                wait(pe, h_add, i)
                for t in range(2):
                    for f in range(2):
                        l = nc.tensor.matmul(pSD[:, t * D:(t + 1) * D],
                                             sh_h[:, par, f * HALF + t * P:f * HALF + (t + 1) * P],
                                             WF[:, F_SD + f * D:F_SD + (f + 1) * D], start=(f == 0), stop=(f == 1))
                l.then_inc(h_d, 1)

            def body(it, first):
                for j in range(BODY):
                    n = it * BODY + j
                    if j % 5 == 0:
                        shared_gu(it * 2 + j // 5)
                    if j % 5 == 2:
                        shared_d(it * 2 + j // 5, j // 5)
                    rows_t(n, it, j)
                    if not (first and j < 1):
                        gate_up(n - 1, (j - 1) % BODY)
                    if not (first and j < 2):
                        hidden_t(n - 2, (j - 2) % BODY)
                    if not (first and j < 3):
                        down(n - 3, (j - 3) % BODY)

            pe.wait_ge(s_wf, 16)
            pe.wait_ge(t_table, 1)
            pe.wait_ge(c_zT2, NQ)
            body(0, True)
            with pe.Fori(1, TURNS) as it:
                body(it, False)
            gate_up(BLOCKS - 1, BODY - 1)
            hidden_t(BLOCKS - 2, BODY - 2)
            down(BLOCKS - 3, BODY - 3)
            hidden_t(BLOCKS - 1, BODY - 1)
            down(BLOCKS - 2, BODY - 2)
            down(BLOCKS - 1, BODY - 1)


def kernel(L0_attn_x, L0_attn_wq, L0_attn_wk, L0_attn_wv, L0_attn_wo, L0_attn_bo, L0_ffn_router_w,
           L0_ffn_gate_up_w, L0_ffn_down_w, L0_ffn_shared_gate_w, L0_ffn_shared_up_w, L0_ffn_shared_down_w):
    import numpy as np
    import concourse.bacc as bacc
    from concourse.bass_utils import run_bass_kernel_spmd

    f32 = np.float32
    t = lambda a: np.asarray(a).T
    w_att = np.ascontiguousarray(np.concatenate(
        [t(L0_attn_wq), t(L0_attn_wk), t(L0_attn_wv), t(L0_attn_wo), t(L0_ffn_router_w)], axis=1))
    gate_up = np.asarray(L0_ffn_gate_up_w).transpose(1, 0, 2).reshape(D, -1)
    down = np.asarray(L0_ffn_down_w).transpose(1, 0, 2).reshape(EXP_DIM, -1)
    s_down = t(L0_ffn_shared_down_w).reshape(SHARED // P, P, D).transpose(1, 0, 2).reshape(P, -1)
    w_ffn = np.ascontiguousarray(np.concatenate(
        [gate_up, down, t(L0_ffn_shared_gate_w), t(L0_ffn_shared_up_w), s_down], axis=1))
    i, c = np.arange(P)[:, None], np.arange(P)[None, :]
    e = np.arange(EXPERTS)[None, :]
    consts = np.zeros((P, C_ALL), f32)
    consts[:, C_IDENT:C_IDENT + P] = i == c
    consts[:, C_TRI:C_TRI + P] = i < c
    consts[:, C_MASK:C_MASK + D] = i // HD == c // HD
    consts[:, C_MASK + D:C_MASK + RK] = i // HD == e
    consts[:, C_IOTA:C_IOTA + EXPERTS] = e
    consts[:, C_BASE:C_BASE + EXPERTS] = e * REGION
    consts[:, C_SLOT:C_SLOT + 1] = i
    consts[0:EXPERTS, C_CUM:C_CUM + EXPERTS] = i[:EXPERTS] <= e
    consts[0:EXPERTS, C_CUM + EXPERTS:C_ALL] = i[:EXPERTS] == e
    q, b, j, k = np.meshgrid(np.arange(NQ), np.arange(SPQ), np.arange(2), np.arange(TOP_K), indexing="ij")
    tokid = (k * TOKENS + q * QTOK + b * SEQ + j).reshape(1, -1) + 2 * i
    arrays = {
        "x": np.ascontiguousarray(np.asarray(L0_attn_x).reshape(TOKENS, D)),
        "w_att": w_att,
        "bo": np.ascontiguousarray(np.asarray(L0_attn_bo).reshape(1, D)),
        "w_ffn": w_ffn,
        "consts": consts,
        "tokid": tokid.astype(np.uint32),
    }
    nc = bacc.Bacc("TRN2", target_bir_lowering=False, num_devices=1)
    args = [nc.dram_tensor(n, a.shape, mybir.dt.from_np(a.dtype), kind="ExternalInput").ap() for n, a in arrays.items()]
    out = nc.dram_tensor("out", (TOKENS, D), mybir.dt.float32, kind="ExternalOutput").ap()
    preln_block(nc, *args, out)
    r = run_bass_kernel_spmd(nc, [arrays], core_ids=[0])
    return r.results[0]["out"].reshape(BATCHES, SEQ, D)
```

```python
import concourse.bass as bass
from concourse import mybir
from contextlib import ExitStack

P = 128
D = 128
HEADS = 16
HD = D // HEADS
BATCHES, SEQ = 16, 256
TOKENS = BATCHES * SEQ
EXPERTS, TOP_K = 16, 2
EXP_DIM = 128
SHARED = 256
LN_EPS, ATT_EPS = 1e-5, 1e-6

QUAD = 4
QTOK = QUAD * P
NQ = TOKENS // QTOK
SPQ = QTOK // SEQ
RK = D + HEADS

REGION = TOKENS + P
REGION_BLOCKS = REGION // P
ROW = D + 2
SKIP = 1 << 20
PAIRS = TOP_K * TOKENS
MAX_BLOCKS = PAIRS // P + EXPERTS - 1
BODY = 16
TURNS = -(-MAX_BLOCKS // BODY)
BLOCKS = TURNS * BODY
HALF = 2 * P
HALVES = TOKENS // HALF
AHEAD = 5
AFTER = AHEAD + TURNS
LEAD = 4

C_IDENT, C_TRI, C_MASK = 0, P, 2 * P
C_IOTA = C_MASK + RK
C_BASE = C_IOTA + EXPERTS
C_SLOT = C_BASE + EXPERTS
C_CUM = C_SLOT + 1
C_ALL = C_CUM + 2 * EXPERTS
W_Q, W_KV, W_O, W_R = 0, D, 3 * D, 4 * D
W_ALL = 4 * D + EXPERTS
F_GU = 0
F_DN = EXPERTS * 2 * EXP_DIM
F_SG = F_DN + EXPERTS * D
F_SU = F_SG + SHARED
F_SD = F_SU + SHARED
F_ALL = F_SD + SHARED // P * D


def preln_block(nc, x, w_att, bo, w_ffn, consts, tokid, out):
    F32, BF16 = mybir.dt.float32, mybir.dt.bfloat16
    U32, I32 = mybir.dt.uint32, mybir.dt.int32
    ALU, ACT, AX = mybir.AluOpType, mybir.ActivationFunctionType, mybir.AxisListType

    x_v = x.rearrange("(q b p j) c -> q p b (j c)", b=SPQ, p=P, j=2)
    out_v = out.rearrange("(q b p j) c -> q p b (j c)", b=SPQ, p=P, j=2)

    with ExitStack() as ctx:
        def sb(name, shape, dt=F32):
            return ctx.enter_context(nc.sbuf_tensor(name, shape, dt))

        def pb(name, shape):
            return ctx.enter_context(nc.psum_tensor(name, shape, F32))

        def sem(name):
            return ctx.enter_context(nc.semaphore(name))

        routed = nc.dram_tensor("routed", ((EXPERTS + 1) * REGION, ROW), F32, kind="Internal").ap()
        results = nc.dram_tensor("results", (PAIRS, D), F32, kind="Internal").ap()
        res_v = results.rearrange("(k q b p j) c -> k q p b (j c)", k=TOP_K, b=SPQ, p=P, j=2)

        X = sb("X", [P, NQ * QTOK])
        X1 = sb("X1", [P, NQ * QTOK])
        ZT = sb("ZT", [P, NQ * QTOK])
        WA = sb("WA", [P, W_ALL])
        WF = sb("WF", [P, F_ALL])
        CN = sb("CN", [P, C_ALL])
        TOK = sb("TOK", [P, NQ * QUAD * TOP_K], U32)
        bo_row = sb("bo_row", [1, D])
        bo_all = sb("bo_all", [P, D])
        ones_row = sb("ones_row", [1, P])
        ones = sb("ones", [P, P], BF16)
        tri = sb("tri", [P, P], BF16)
        eps = sb("eps", [P, 1])
        ident = CN[:, C_IDENT:C_IDENT + P]

        a_stat = sb("a_stat", [P, QUAD, 6])
        a_mv = sb("a_mv", [P, QUAD, 2])
        a_rs = sb("a_rs", [P, 6, QUAD])
        XN = sb("XN", [P, 2, QUAD, D])
        XNT = sb("XNT", [P, 2, QTOK])
        rq = sb("rq", [P, QTOK])
        eq = sb("eq", [P, QTOK])
        rk = sb("rk", [P, QUAD, D])
        ek = sb("ek", [P, QUAD, D])
        QF = sb("QF", [P, 2, QTOK])
        KF = sb("KF", [P, 2, QUAD, D])
        V = sb("V", [P, 2, QUAD, D + 4])
        KV = sb("KV", [P, SPQ, RK])
        den = sb("den", [P, QUAD, HEADS])
        rden = sb("rden", [P, QUAD, HEADS])
        att = sb("att", [P, QUAD, D])
        attT = sb("attT", [P, QTOK])
        c_stat = sb("c_stat", [P, QUAD, 6])
        c_mv = sb("c_mv", [P, QUAD, 2])
        c_rs = sb("c_rs", [P, 6, QUAD])
        Z = sb("Z", [P, 2, QUAD, TOP_K, ROW])
        zT = sb("zT", [P, QTOK])
        top = sb("top", [P, QUAD, 8])
        top_i = sb("top_i", [P, QUAD, 8], U32)
        onehot = sb("onehot", [P, QUAD, TOP_K, EXPERTS])
        chosen = sb("chosen", [P, QUAD, EXPERTS], BF16)
        chosen_q = sb("chosen_q", [P, EXPERTS], BF16)
        chosen_all = sb("chosen_all", [P, EXPERTS], BF16)
        slot = sb("slot", [P, QUAD, EXPERTS])
        slot_k = sb("slot_k", [P, QUAD, TOP_K, EXPERTS])
        ROWS = sb("ROWS", [P, 2, QUAD, TOP_K], U32)
        gate_e = sb("gate_e", [P, QUAD, TOP_K])
        gate_1 = sb("gate_1", [P, QUAD, TOP_K])
        pad = sb("pad", [P, ROW])
        pad_at = sb("pad_at", [1, EXPERTS], I32)
        nb_a = sb("nb_a", [EXPERTS, P], I32)
        nb_b = sb("nb_b", [EXPERTS, P], I32)
        nb = sb("nb", [EXPERTS, P])
        before = sb("before", [P, EXPERTS])
        before_nb = sb("before_nb", [P, EXPERTS])
        blk = sb("blk", [P, 8])
        table_f = sb("table_f", [P, 2])
        table_b = sb("table_b", [1, LEAD + P], I32)
        table_e = sb("table_e", [1, LEAD + P], I32)
        XS = sb("XS", [P, BODY, ROW])
        Y = sb("Y", [P, BODY, D])
        xT = sb("xT", [P, 2, P])
        sg = sb("sg", [P, 2, EXP_DIM])
        h = sb("h", [P, 2, EXP_DIM])
        hT = sb("hT", [P, 2, P])
        sh_s = sb("sh_s", [P, 2 * HALF])
        sh_h = sb("sh_h", [P, 2 * HALF])
        YL = sb("YL", [P, 2, TOP_K, QTOK])
        ysum = sb("ysum", [P, 2, QTOK])

        pT = pb("pT", [P, 512])
        pQ = pb("pQ", [P, 512])
        pKVN = pb("pKVN", [P, QUAD, 256])
        pKV = pb("pKV", [P, 2, 256])
        pN = pb("pN", [P, QUAD, 256])
        pZ = pb("pZ", [P, 512])
        pO = pN[:, 0:2, :].rearrange("p a c -> p (a c)")
        pAT = pKV[:, :, :].rearrange("p a c -> p (a c)")
        pL = pZ[:, 0:QUAD * EXPERTS].rearrange("p (t e) -> p t e", e=EXPERTS)
        pR = pZ[:, 128:128 + QUAD * EXPERTS].rearrange("p (t e) -> p t e", e=EXPERTS)
        pX = pT[:, 0:P]
        pGU = [pQ, pZ]
        pHT = pKV[:, 0, 0:P]
        pY = pKVN[:, 0, 0:D]
        pSG = pKVN[:, 2:4, :].rearrange("p a c -> p (a c)")
        pSU = pN[:, 0:2, :].rearrange("p a c -> p (a c)")
        pSD = pN[:, 2, :]

        s_cn, s_wa, s_wf = sem("s_cn"), sem("s_wa"), sem("s_wf")
        waited = sem("waited")
        s_x = sem("s_x")
        s_ones, s_tri, s_bo, s_bo_all = sem("s_ones"), sem("s_tri"), sem("s_bo"), sem("s_bo_all")
        s_xb = sem("s_xb")
        a_stats, a_aggr, a_rstd, a_norm = sem("a_stats"), sem("a_aggr"), sem("a_rstd"), sem("a_norm")
        a_ln, a_y, a_n1, a_n2 = sem("a_ln"), sem("a_y"), sem("a_n1"), sem("a_n2")
        a_shift = sem("a_shift")
        c_ln, c_y, c_n1, c_n2 = sem("c_ln"), sem("c_y"), sem("c_n1"), sem("c_n2")
        a_T, a_xT, a_q, a_kv = sem("a_T"), sem("a_xT"), sem("a_q"), sem("a_kv")
        a_rk, a_ek, a_rq, a_eq, a_v = sem("a_rk"), sem("a_ek"), sem("a_rq"), sem("a_eq"), sem("a_v")
        a_kf, a_qf = sem("a_kf"), sem("a_qf")
        b_kv, b_mask1, b_mask, b_num = sem("b_kv"), sem("b_mask1"), sem("b_mask"), sem("b_num")
        b_den, b_rden, b_att = sem("b_den"), sem("b_rden"), sem("b_att")
        b_T, b_aT, b_wo = sem("b_T"), sem("b_aT"), sem("b_wo")
        c_x1, c_stats, c_aggr, c_rstd = sem("c_x1"), sem("c_stats"), sem("c_aggr"), sem("c_rstd")
        c_z, c_zdup, c_T, c_zT, c_zT2 = sem("c_z"), sem("c_zdup"), sem("c_T"), sem("c_zT"), sem("c_zT2")
        c_lg, c_top, c_idx = sem("c_lg"), sem("c_top"), sem("c_idx")
        c_oh, c_ch, c_rank, c_chq, c_cha = sem("c_oh"), sem("c_ch"), sem("c_rank"), sem("c_chq"), sem("c_cha")
        c_slot, c_slotk, c_rows = sem("c_slot"), sem("c_slotk"), sem("c_rows")
        c_ge, c_g1, c_pay = sem("c_ge"), sem("c_g1"), sem("c_pay")
        scat = [sem("scat0"), sem("scat1")]
        t_cnt, t_nba, t_nbb, t_nb, t_cum = sem("t_cnt"), sem("t_nba"), sem("t_nbb"), sem("t_nb"), sem("t_cum")
        t_v, t_tab, t_row, t_table, t_pad, t_pads = (sem("t_v"), sem("t_tab"), sem("t_row"),
                                                     sem("t_table"), sem("t_pad"), sem("t_pads"))
        xs = [sem(f"xs{j}") for j in range(BODY)]
        ysc = [sem(f"ysc{j}") for j in range(BODY)]
        s_Tx, s_xT, s_gu, s_silu, s_h = sem("s_Tx"), sem("s_xT"), sem("s_gu"), sem("s_silu"), sem("s_h")
        s_Th, s_hT, s_D, s_y = sem("s_Th"), sem("s_hT"), sem("s_D"), sem("s_y")
        h_gu, h_silu, h_h, h_d, h_add = sem("h_gu"), sem("h_silu"), sem("h_h"), sem("h_d"), sem("h_add")
        yl = [sem("yl0"), sem("yl1")]
        c_sum, c_out, s_out = sem("c_sum"), sem("c_out"), sem("s_out")

        def wait(eng, semaphore, count):
            if not isinstance(count, int) or count > 0:
                eng.wait_ge(semaphore, count)

        def quad(t, q):
            return t[:, bass.ds(q * QTOK, QTOK)]

        def steps(eng, step):
            for s in range(4):
                step(s, s % 2)
            with eng.Fori(0, 1) as it:
                for u in range(2):
                    step(it * 2 + (4 + u), (4 + u) % 2)
            for s in range(6, NQ + 3):
                step(s, s % 2)

        def wait_apart(eng, semaphore, count):
            eng.wait_ge(semaphore, count)
            eng.sem_inc(waited, 1)

        def has(s, lag):
            return not isinstance(s, int) or 0 <= s - lag < NQ

        def values(eng, row, start, count, most):
            return nc.values_load_multi_w_load_instructions(
                row[0:1, bass.ds(start, count)], engines=(eng.engine,), min_val=0, max_val=most,
                skip_runtime_bounds_check_because="the table is clamped where it is made")[1]

        def pads(eng, half):
            n = EXPERTS // 2
            for at in values(eng, pad_at, half * n, n, EXPERTS * REGION - P):
                eng.dma_start(routed[bass.ds(at, P), :], pad[:, :]).then_inc(t_pads, 16)

        block = ctx.enter_context(nc.Block())

        @block.sync
        def _(sp):
            sp.dma_start(quad(X, 0).rearrange("p (b f) -> p b f", b=SPQ), x_v[0]).then_inc(s_x, 16)
            sp.dma_start(bo_row[0:1, :], bo).then_inc(s_bo, 16)
            sp.wait_ge(s_x, 16)
            with sp.Fori(1, NQ) as q:
                sp.dma_start(quad(X, q).rearrange("p (b f) -> p b f", b=SPQ),
                             x_v[bass.ds(q, 1)].rearrange("o p b f -> (o p) b f")).then_inc(s_x, 16)
                wait_apart(sp, s_x, q * 16 + 16)

            sp.wait_ge(t_pad, 2)
            pads(sp, 0)
            sp.dma_start(routed[EXPERTS * REGION:EXPERTS * REGION + P, :], pad[:, :]).then_inc(t_pads, 16)
            sp.wait_ge(t_pads, 16 * (EXPERTS + 1))
            for s_ in scat:
                sp.wait_ge(s_, 16 * QUAD * TOP_K * NQ // 2)
            sp.wait_ge(t_table, 2)

            def load(it):
                at = values(sp, table_b, it * BODY + LEAD, BODY, EXPERTS * REGION_BLOCKS)
                for j in range(BODY):
                    wait(sp, ysc[j], it * 16)
                    sp.dma_start(XS[:, j, :], routed[bass.ds(at[j] * P, P), :]).then_inc(xs[j], 16)

            load(0)
            with sp.Fori(1, TURNS) as it:
                load(it)

            for s_ in ysc:
                sp.wait_ge(s_, 16 * TURNS)

            def load_y(q, par):
                for k in range(TOP_K):
                    sp.dma_start(YL[:, par, k, :].rearrange("p (b f) -> p b f", b=SPQ),
                                 res_v[k, bass.ds(q, 1)].rearrange("o p b f -> (o p) b f")
                                 ).then_inc(yl[par], 16)

            for q in range(2):
                load_y(q, q)
            with sp.Fori(1, NQ // 2) as it:
                for par in range(2):
                    sp.wait_ge(c_sum, it * 2 + (par - 1))
                    load_y(it * 2 + par, par)
            sp.wait_ge(s_out, 16 * NQ)

        @block.gpsimd
        def _(pool):
            pool.wait_ge(s_bo_all, 2)
            bo_q = bo_all[:, :].unsqueeze(1).to_broadcast([P, QUAD, D])
            with pool.Fori(0, NQ) as q:
                pool.wait_ge(s_x, q * 16 + 16)
                nc.gpsimd.tensor_tensor(quad(X1, q).rearrange("p (t c) -> p t c", t=QUAD),
                                        quad(X, q).rearrange("p (t c) -> p t c", t=QUAD),
                                        bo_q, ALU.add).then_inc(s_xb, 1)

            def dispatch(q, par):
                pool.wait_ge(c_rows, q + 1)
                pool.wait_ge(c_pay, q + 1)
                wait_apart(pool, c_zdup, q + 1)
                for t in range(QUAD):
                    for k in range(TOP_K):
                        nc.gpsimd.indirect_dma_start(
                            routed, bass.IndirectOffsetOnAxis(ap=ROWS[:, par, t, k:k + 1], axis=0),
                            Z[:, par, t, k, :], None).then_inc(scat[par], 16)

            with pool.Fori(0, NQ // 2) as it:
                for par in range(2):
                    dispatch(it * 2 + par, par)

            with pool.Fori(0, TURNS) as it:
                for j in range(BODY):
                    wait_apart(pool, s_y, it * BODY + (j + 1))
                    nc.gpsimd.indirect_dma_start(
                        results, bass.IndirectOffsetOnAxis(ap=XS[:, j, D:D + 1].bitcast(U32), axis=0),
                        Y[:, j, :], None, bounds_check=PAIRS - 1, oob_is_err=False).then_inc(ysc[j], 16)

            with pool.Fori(0, NQ // 2) as it:
                for par in range(2):
                    pool.wait_ge(yl[par], it * 32 + 32)
                    nc.gpsimd.tensor_tensor(ysum[:, par, :], YL[:, par, 0, :], YL[:, par, 1, :],
                                            ALU.add).then_inc(c_sum, 1)
                    pool.wait_ge(c_out, it * 2 + (par + 1))

        @block.scalar
        def _(act):
            act.dma_start(CN[:, :], consts).then_inc(s_cn, 16)
            act.dma_start(WA[:, :], w_att).then_inc(s_wa, 16)
            act.dma_start(TOK[:, :], tokid).then_inc(s_cn, 16)
            act.dma_start(WF[:, :], w_ffn).then_inc(s_wf, 16)

            def rstd(mv, rs, aggr, ln, y, q):
                act.wait_ge(aggr, q + 1)
                nc.scalar.activation(rs[:, 0, :], mv[:, :, 1], ACT.Ln, bias=eps[:, 0:1]).then_inc(ln, 1)
                act.wait_ge(ln, q + 1)
                nc.scalar.activation(rs[:, 1, :], rs[:, 0, :], ACT.Exp, scale=-0.5).then_inc(y, 1)

            act.preload_act_table_set("natural_log_exp_and_others")
            rstd(a_mv, a_rs, a_aggr, a_ln, a_y, 0)

            def norm1(q, par):
                act.wait_ge(a_shift, q + 1)
                wait(act, a_T, q - 1)
                for t in range(QUAD):
                    i = nc.scalar.activation(XN[:, par, t, :], X[:, bass.ds(q * QTOK + t * D, D)], ACT.Identity,
                                             bias=a_rs[:, 5, t:t + 1], scale=a_rs[:, 4, t:t + 1])
                i.then_inc(a_norm, 1)

            norm1(0, 0)

            def tokens_t(q, par):
                act.wait_ge(a_T, q + 1)
                wait(act, a_kv, q - 1)
                nc.scalar.copy(XNT[:, par, :], pT[:, :]).then_inc(a_xT, 1)

            tokens_t(0, 0)

            def step(s, par):
                this, att_, last, coming = has(s, 0), has(s, 1), has(s, 2), has(s, -1)
                if this:
                    act.wait_ge(a_q, s + 1)
                    nc.scalar.activation(rq[:, :], pQ[:, :], ACT.Relu, scale=-1.0).then_inc(a_rq, 1)
                    act.wait_ge(a_rq, s + 1)
                    wait(act, a_qf, s)
                    nc.scalar.activation(eq[:, :], rq[:, :], ACT.Exp, scale=-1.0).then_inc(a_eq, 1)
                if last:
                    rstd(c_mv, c_rs, c_aggr, c_ln, c_y, s - 2)
                if coming:
                    rstd(a_mv, a_rs, a_aggr, a_ln, a_y, s + 1)
                if this:
                    act.wait_ge(a_kv, s + 1)
                    nc.scalar.activation(rk[:, :, :], pKVN[:, :, 0:D], ACT.Relu, scale=-1.0).then_inc(a_rk, 1)
                if last:
                    q = s - 2
                    act.wait_ge(c_T, q + 1)
                    wait(act, c_lg, q)
                    nc.scalar.copy(zT[:, :], pZ[:, :]).then_inc(c_zT, 1)
                if this:
                    wait(act, b_kv, s - 1)
                    nc.scalar.copy(V[:, par, :, 0:D], pKVN[:, :, D:2 * D]).then_inc(a_v, 1)
                    act.wait_ge(a_rk, s + 1)
                    wait(act, a_kf, s)
                    nc.scalar.activation(ek[:, :, :], rk[:, :, :], ACT.Exp, scale=-1.0).then_inc(a_ek, 1)
                if att_:
                    q = s - 1
                    act.wait_ge(b_T, q + 1)
                    wait(act, b_wo, q)
                    nc.scalar.copy(attT[:, :], pAT).then_inc(b_aT, 1)
                if coming:
                    norm1(s + 1, 1 - par)
                if last:
                    q = s - 2
                    act.wait_ge(c_top, q + 1)
                    wait(act, c_g1, q)
                    nc.scalar.activation(gate_e[:, :, :], top[:, :, 0:TOP_K], ACT.Exp, scale=-1.0).then_inc(c_ge, 1)
                    act.wait_ge(c_z, q + 1)
                    nc.scalar.copy(Z[:, par, :, 1, 0:D], Z[:, par, :, 0, 0:D]).then_inc(c_zdup, 1)
                if coming:
                    tokens_t(s + 1, 1 - par)
                if last:
                    q = s - 2
                    act.wait_ge(c_zT, q + 1)
                    nc.scalar.copy(quad(ZT, q), zT[:, :]).then_inc(c_zT2, 1)

            steps(act, step)

            def silu(n, j):
                act.wait_ge(s_gu, n + 1)
                wait(act, s_h, n - 1)
                nc.scalar.activation(sg[:, j % 2, :], pGU[j % 2][:, 0:EXP_DIM], ACT.Silu).then_inc(s_silu, 1)

            def scaled(n, j):
                act.wait_ge(s_D, n + 1)
                nc.scalar.activation(Y[:, j, :], pY, ACT.Copy, scale=XS[:, j, D + 1:D + 2]).then_inc(s_y, 1)

            def shared(i):
                act.wait_ge(h_gu, i + 1)
                wait(act, h_h, i)
                nc.scalar.activation(sh_s[:, :], pSG, ACT.Silu).then_inc(h_silu, 1)

            shared(0)
            act.wait_ge(t_pad, 2)
            pads(act, 1)
            with act.Fori(1, AHEAD) as i:
                shared(i)

            def body(it, first):
                for j in range(BODY):
                    n = it * BODY + j
                    if j == 2:
                        shared(it + AHEAD)
                    if not (first and j < 1):
                        silu(n - 1, (j - 1) % BODY)
                    if not (first and j < 3):
                        scaled(n - 3, (j - 3) % BODY)

            body(0, True)
            with act.Fori(1, TURNS) as it:
                body(it, False)
            silu(BLOCKS - 1, BODY - 1)
            for k in range(3):
                scaled(BLOCKS - 3 + k, BODY - 3 + k)

            def store(q):
                act.wait_ge(c_out, q + 1)
                act.dma_start(out_v[bass.ds(q, 1)].rearrange("o p b f -> (o p) b f"),
                              quad(X1, q).rearrange("p (b f) -> p b f", b=SPQ)).then_inc(s_out, 16)

            shared(AFTER)
            shared(AFTER + 1)
            with act.Fori(0, HALVES - AFTER - 2) as q:
                shared(q + (AFTER + 2))
                store(q)
            with act.Fori(HALVES - AFTER - 2, NQ) as q:
                store(q)

        @block.vector
        def _(dve):
            nc.vector.memset(ones_row[:, :], 1.0)
            nc.vector.memset(ones[:, :], 1.0)
            nc.vector.memset(chosen_all[:, :], 0.0)
            nc.vector.memset(table_e[0:1, 0:LEAD], 0).then_inc(t_table, 1)
            nc.vector.memset(eps[:, :], LN_EPS)
            nc.vector.memset(pad[:, :], 0.0).then_inc(t_pad, 1)
            nc.vector.memset(V[:, :, :, D:D + 1], 1.0).then_inc(s_ones, 1)
            dve.wait_ge(t_pad, 1)
            nc.vector.memset(pad[:, D:D + 1].bitcast(U32), SKIP).then_inc(s_ones, 1)
            dve.wait_ge(s_cn, 32)
            nc.vector.tensor_copy(tri[:, :], CN[:, C_TRI:C_TRI + P]).then_inc(s_tri, 1)
            dve.wait_ge(s_bo_all, 1)
            nc.vector.tensor_copy(bo_all[:, :], pQ[:, 0:D]).then_inc(s_bo_all, 1)

            def bn_stats(src, stat, stats, q):
                for t in range(QUAD):
                    i = nc.vector.bn_stats(stat[:, t, :], src[:, bass.ds(q * QTOK + t * D, D)])
                i.then_inc(stats, 1)

            def bn_aggr(stat, mv, stats, aggr, q):
                wait_apart(dve, stats, q + 1)
                for t in range(QUAD):
                    i = nc.vector.bn_aggr(mv[:, t, :], stat[:, t, :])
                i.then_inc(aggr, 1)

            def newton1(mv, rs, y, n1, q):
                dve.wait_ge(y, q + 1)
                nc.vector.scalar_tensor_tensor(rs[:, 2, :], mv[:, :, 1], LN_EPS, rs[:, 1, :], ALU.add, ALU.mult).then_inc(n1, 1)

            def newton2(rs, n1, n2, q):
                dve.wait_ge(n1, q + 1)
                nc.vector.scalar_tensor_tensor(rs[:, 3, :], rs[:, 2, :], -0.5, rs[:, 1, :], ALU.mult, ALU.mult).then_inc(n2, 1)

            def newton3(rs, n2, rstd, q):
                dve.wait_ge(n2, q + 1)
                nc.vector.scalar_tensor_tensor(rs[:, 4, :], rs[:, 3, :], 1.5, rs[:, 1, :], ALU.add, ALU.mult).then_inc(rstd, 1)

            def shift1(q):
                dve.wait_ge(a_rstd, q + 1)
                nc.vector.scalar_tensor_tensor(a_rs[:, 5, :], a_mv[:, :, 0], -1.0, a_rs[:, 4, :], ALU.mult, ALU.mult).then_inc(a_shift, 1)

            def residual(q):
                dve.wait_ge(b_wo, q + 1)
                dve.wait_ge(s_xb, q + 1)
                nc.vector.tensor_tensor(quad(X1, q), pO, quad(X1, q), ALU.add).then_inc(c_x1, 1)

            def norm2(q, par, turn):
                dve.wait_ge(c_rstd, q + 1)
                wait(dve, scat[par], turn)
                for t in range(QUAD):
                    i = nc.vector.tensor_scalar(Z[:, par, t, 0, 0:D], X1[:, bass.ds(q * QTOK + t * D, D)],
                                                c_mv[:, t, 0:1], c_rs[:, 4, t:t + 1], ALU.subtract, ALU.mult)
                i.then_inc(c_z, 1)

            def mask(q):
                dve.wait_ge(b_kv, q + 1)
                wait(dve, b_num, q)
                nc.vector.tensor_tensor(
                    KV[:, :, 0:D], pKV[:, :, 0:D],
                    CN[:, C_MASK:C_MASK + D].unsqueeze(1).to_broadcast([P, SPQ, D]), ALU.mult).then_inc(b_mask1, 1)
                nc.vector.tensor_tensor(
                    KV[:, :, D:RK], pKV[:, :, D:D + 1].to_broadcast([P, SPQ, HEADS]),
                    CN[:, C_MASK + D:C_MASK + RK].unsqueeze(1).to_broadcast([P, SPQ, HEADS]),
                    ALU.mult).then_inc(b_mask, 1)

            def attend1(q):
                dve.wait_ge(b_num, q + 1)
                nc.vector.tensor_scalar(den[:, :, :], pN[:, :, D:RK], ATT_EPS, None, ALU.add).then_inc(b_den, 1)
                dve.wait_ge(b_den, q + 1)
                nc.vector.reciprocal(rden[:, :, :], den[:, :, :]).then_inc(b_rden, 1)

            def attend2(q):
                dve.wait_ge(b_rden, q + 1)
                wait(dve, b_T, q)
                nc.vector.tensor_tensor(
                    att[:, :, :].rearrange("p t (h d) -> p t h d", d=HD),
                    pN[:, :, 0:D].rearrange("p t (h d) -> p t h d", d=HD),
                    rden[:, :, :].unsqueeze(3).to_broadcast([P, QUAD, HEADS, HD]), ALU.mult).then_inc(b_att, 1)

            def features_q(q, par):
                dve.wait_ge(a_eq, q + 1)
                wait(dve, b_num, q - 1)
                nc.vector.scalar_tensor_tensor(QF[:, par, :], pQ[:, :], 1.0, eq[:, :], ALU.add, ALU.max).then_inc(a_qf, 1)

            def features_k(q, par):
                dve.wait_ge(a_ek, q + 1)
                wait(dve, b_kv, q - 1)
                nc.vector.scalar_tensor_tensor(KF[:, par, :, :], pKVN[:, :, 0:D], 1.0, ek[:, :, :],
                                               ALU.add, ALU.max).then_inc(a_kf, 1)

            def route(q, par):
                wait_apart(dve, c_lg, q + 1)
                for t in range(QUAD):
                    i = nc.vector.max(top[:, t, :], pL[:, t, :])
                i.then_inc(c_top, 1)
                nc.vector.tensor_copy(Z[:, par, :, :, D].bitcast(U32),
                                      TOK[:, bass.ds(q * QUAD * TOP_K, QUAD * TOP_K)].rearrange("p (t k) -> p t k", k=TOP_K))
                wait_apart(dve, c_top, q + 1)
                for t in range(QUAD):
                    i = nc.vector.max_index(top_i[:, t, :], top[:, t, :], pL[:, t, :])
                i.then_inc(c_idx, 1)
                dve.wait_ge(c_ge, q + 1)
                nc.vector.tensor_scalar(gate_1[:, :, :], gate_e[:, :, :], 1.0, None, ALU.add).then_inc(c_g1, 1)
                dve.wait_ge(c_idx, q + 1)
                nc.vector.tensor_tensor(
                    onehot[:, :, :, :],
                    CN[:, C_IOTA:C_IOTA + EXPERTS].unsqueeze(1).unsqueeze(1).to_broadcast([P, QUAD, TOP_K, EXPERTS]),
                    top_i[:, :, 0:TOP_K].unsqueeze(3).to_broadcast([P, QUAD, TOP_K, EXPERTS]),
                    ALU.is_equal).then_inc(c_oh, 1)
                dve.wait_ge(c_g1, q + 1)
                nc.vector.reciprocal(Z[:, par, :, :, D + 1], gate_1[:, :, :]).then_inc(c_pay, 1)
                dve.wait_ge(c_oh, q + 1)
                nc.vector.tensor_tensor(chosen[:, :, :], onehot[:, :, 0, :], onehot[:, :, 1, :], ALU.add).then_inc(c_ch, 1)
                dve.wait_ge(c_ch, q + 1)
                with nc.allow_low_precision("counts up to 32 are exact in bfloat16"):
                    nc.vector.tensor_reduce(chosen_q[:, :], chosen[:, :, :].rearrange("p t e -> p e t"), AX.X, ALU.add).then_inc(c_chq, 1)

            def rows1(q):
                dve.wait_ge(c_rank, q + 1)
                nc.vector.tensor_tensor(
                    slot[:, :, :], pR,
                    CN[:, C_BASE:C_BASE + EXPERTS].unsqueeze(1).to_broadcast([P, QUAD, EXPERTS]), ALU.add).then_inc(c_slot, 1)
                dve.wait_ge(c_chq, q + 1)
                nc.vector.tensor_tensor(chosen_all[:, :], chosen_all[:, :], chosen_q[:, :], ALU.add).then_inc(c_cha, 1)

            def rows2(q):
                dve.wait_ge(c_slot, q + 1)
                nc.vector.tensor_tensor(slot_k[:, :, :, :], onehot[:, :, :, :],
                                        slot[:, :, :].unsqueeze(2).to_broadcast([P, QUAD, TOP_K, EXPERTS]),
                                        ALU.mult).then_inc(c_slotk, 1)

            def rows3(q, par):
                dve.wait_ge(c_slotk, q + 1)
                with nc.allow_low_precision("row numbers are whole and below 2 ** 24"):
                    nc.vector.tensor_reduce(ROWS[:, par, :, :], slot_k[:, :, :, :], AX.X, ALU.add).then_inc(c_rows, 1)

            def step(s, par):
                this, att_, last, tail, coming = has(s, 0), has(s, 1), has(s, 2), has(s, 3), has(s, -1)
                if last:
                    residual(s - 2)
                    wait_apart(dve, c_x1, s - 1)
                    bn_stats(X1, c_stat, c_stats, s - 2)
                    bn_aggr(c_stat, c_mv, c_stats, c_aggr, s - 2)
                if tail:
                    rows1(s - 3)
                if att_:
                    mask(s - 1)
                if tail:
                    rows2(s - 3)
                if coming:
                    wait_apart(dve, s_x, (s + 1) * 16 + 16)
                    bn_stats(X, a_stat, a_stats, s + 1)
                if tail:
                    rows3(s - 3, 1 - par)
                if coming:
                    bn_aggr(a_stat, a_mv, a_stats, a_aggr, s + 1)
                if last:
                    newton1(c_mv, c_rs, c_y, c_n1, s - 2)
                if this:
                    features_q(s, par)
                if last:
                    newton2(c_rs, c_n1, c_n2, s - 2)
                if coming:
                    newton1(a_mv, a_rs, a_y, a_n1, s + 1)
                if last:
                    newton3(c_rs, c_n2, c_rstd, s - 2)
                if coming:
                    newton2(a_rs, a_n1, a_n2, s + 1)
                if last:
                    q = s - 2
                    turn = (q // 2) * 128 if isinstance(q, int) else dve_turn(s, par)
                    norm2(q, par, turn)
                if coming:
                    newton3(a_rs, a_n2, a_rstd, s + 1)
                if att_:
                    attend1(s - 1)
                if coming:
                    shift1(s + 1)
                if att_:
                    attend2(s - 1)
                if this:
                    features_k(s, par)
                if last:
                    route(s - 2, par)

            def dve_turn(s, par):
                q = s - 2
                return (q - 1) * 64 if par == 1 else q * 64

            wait_apart(dve, s_x, 16)
            bn_stats(X, a_stat, a_stats, 0)
            bn_aggr(a_stat, a_mv, a_stats, a_aggr, 0)
            newton1(a_mv, a_rs, a_y, a_n1, 0)
            newton2(a_rs, a_n1, a_n2, 0)
            newton3(a_rs, a_n2, a_rstd, 0)
            shift1(0)
            dve.wait_ge(s_tri, 1)
            steps(dve, step)

            def rows(n, j):
                dve.wait_ge(s_Tx, n + 1)
                wait(dve, s_gu, n - 1)
                nc.vector.tensor_copy(xT[:, j % 2, :], pX).then_inc(s_xT, 1)

            def hidden(n, j):
                dve.wait_ge(s_silu, n + 1)
                wait(dve, s_Th, n - 1)
                nc.vector.tensor_tensor(h[:, j % 2, :], pGU[j % 2][:, EXP_DIM:2 * EXP_DIM], sg[:, j % 2, :],
                                        ALU.mult).then_inc(s_h, 1)

            def hidden_t(n, j):
                dve.wait_ge(s_Th, n + 1)
                wait(dve, s_D, n - 1)
                nc.vector.tensor_copy(hT[:, j % 2, :], pHT).then_inc(s_hT, 1)

            def shared_h(i):
                dve.wait_ge(h_silu, i + 1)
                wait(dve, h_d, i)
                nc.vector.tensor_tensor(sh_h[:, :], pSU, sh_s[:, :], ALU.mult).then_inc(h_h, 1)

            def shared_add(i):
                dve.wait_ge(h_d, i + 1)
                x1 = X1[:, bass.ds(i * HALF, HALF)]
                nc.vector.tensor_tensor(x1, pSD, x1, ALU.add).then_inc(h_add, 1)

            dve.wait_ge(t_cnt, 1)
            cnt = pZ[0:EXPERTS, 0:P]
            nc.vector.tensor_scalar(nb_a[:, :], cnt, float(P - 1), None, ALU.add).then_inc(t_nba, 1)
            nc.vector.tensor_tensor(pad_at[0:1, :], pZ[0:1, 256:256 + EXPERTS], CN[0:1, C_BASE:C_BASE + EXPERTS],
                                    ALU.add).then_inc(t_pad, 1)
            dve.wait_ge(t_nba, 1)
            nc.vector.tensor_single_scalar(nb_b[:, :], nb_a[:, :], 7, ALU.arith_shift_right).then_inc(t_nbb, 1)
            dve.wait_ge(t_nbb, 1)
            nc.vector.tensor_copy(nb[:, :], nb_b[:, :]).then_inc(t_nb, 1)
            shared_h(0)
            dve.wait_ge(t_cum, 1)
            cum = pZ[:, 0:EXPERTS]
            nbs = pZ[:, EXPERTS:2 * EXPERTS]
            slot_id = CN[:, C_SLOT:C_SLOT + 1]
            nc.vector.tensor_scalar(before[:, :], cum, slot_id, None, ALU.is_le).then_inc(t_v, 1)
            dve.wait_ge(t_v, 1)
            nc.vector.tensor_tensor(before_nb[:, :], before[:, :], nbs, ALU.mult).then_inc(t_v, 1)
            nc.vector.tensor_reduce(blk[:, 0:1], before[:, :], AX.X, ALU.add).then_inc(t_v, 1)
            dve.wait_ge(t_v, 3)
            nc.vector.tensor_reduce(blk[:, 1:2], before_nb[:, :], AX.X, ALU.add).then_inc(t_v, 1)
            nc.vector.tensor_scalar(blk[:, 2:3], blk[:, 0:1], float(REGION_BLOCKS), slot_id, ALU.mult, ALU.add).then_inc(t_v, 1)
            nc.vector.tensor_scalar(table_f[:, 1:2], blk[:, 0:1], float(EXPERTS - 1), None, ALU.min)
            dve.wait_ge(t_v, 5)
            nc.vector.tensor_scalar(table_f[:, 0:1], blk[:, 2:3], blk[:, 1:2], float(EXPERTS * REGION_BLOCKS),
                                    ALU.subtract, ALU.min).then_inc(t_tab, 1)
            shared_h(1)
            dve.wait_ge(t_row, 1)
            nc.vector.tensor_copy(table_b[0:1, LEAD:], pZ[0:1, P:2 * P])
            nc.vector.tensor_copy(table_e[0:1, LEAD:], pZ[0:1, 2 * P:3 * P]).then_inc(t_table, 1)

            shared_add(0)
            with dve.Fori(1, AHEAD - 1) as i:
                shared_h(i + 1)
                shared_add(i)
            shared_add(AHEAD - 1)

            def body(it, first):
                for j in range(BODY):
                    n = it * BODY + j
                    if j == 2:
                        shared_h(it + AHEAD)
                    if j == 5:
                        shared_add(it + AHEAD)
                    rows(n, j)
                    if not (first and j < 1):
                        hidden(n - 1, (j - 1) % BODY)
                    if not (first and j < 2):
                        hidden_t(n - 2, (j - 2) % BODY)

            body(0, True)
            with dve.Fori(1, TURNS) as it:
                body(it, False)
            hidden(BLOCKS - 1, BODY - 1)
            hidden_t(BLOCKS - 2, BODY - 2)
            hidden_t(BLOCKS - 1, BODY - 1)

            def total(q, par):
                dve.wait_ge(c_sum, q + 1)
                nc.vector.tensor_tensor(quad(X1, q), quad(X1, q), ysum[:, par, :], ALU.add).then_inc(c_out, 1)

            dve.wait_ge(h_add, AFTER)
            shared_h(AFTER)
            with dve.Fori(0, 2) as it:
                for par in range(2):
                    shared_h(it * 2 + (par + AFTER + 1))
                    shared_add(it * 2 + (par + AFTER))
                    total(it * 2 + par, par)
            for q in range(4, NQ):
                i = AFTER + q
                if i + 1 < HALVES:
                    shared_h(i + 1)
                if i < HALVES:
                    shared_add(i)
                dve.wait_ge(h_add, min(2 * q + 2, i + 1))
                total(q, q % 2)

        @block.tensor
        def _(pe):
            pe.wait_ge(s_ones, 2)
            pe.wait_ge(s_bo, 16)
            pe.wait_ge(s_cn, 32)
            pe.wait_ge(s_wa, 16)

            def tokens_t(q, par):
                pe.wait_ge(a_norm, q + 1)
                wait(pe, a_xT, q)
                for t in range(QUAD):
                    i = nc.tensor.transpose(pT[:, t * P:(t + 1) * P], XN[:, par, t, :], ident)
                i.then_inc(a_T, 1)

            def step(s, par):
                par1 = 1 - par
                if has(s, 1):
                    q = s - 1
                    pe.wait_ge(a_kf, q + 1)
                    pe.wait_ge(a_v, q + 1)
                    wait(pe, b_aT, q)
                    for b in range(SPQ):
                        for j in range(2):
                            i = nc.tensor.matmul(pKV[:, b, 0:D + 1], KF[:, par1, 2 * b + j, :],
                                                 V[:, par1, 2 * b + j, 0:D + 1], start=(j == 0), stop=(j == 1))
                    i.then_inc(b_kv, 1)
                if has(s, 0):
                    pe.wait_ge(a_xT, s + 1)
                    wait(pe, a_qf, s)
                    nc.tensor.matmul(pQ[:, :], WA[:, W_Q:W_Q + D], XNT[:, par, :], start=True, stop=True).then_inc(a_q, 1)
                if has(s, 3):
                    q = s - 3
                    pe.wait_ge(c_ch, q + 1)
                    wait(pe, c_cha, q)
                    nc.tensor.matmul(pR, tri[:, :], chosen[:, :, :], start=True, stop=False)
                    for t in range(QUAD - 1):
                        nc.tensor.matmul(pR[:, t + 1:QUAD, :], ones[:, :],
                                         chosen[:, t:t + 1, :].to_broadcast([P, QUAD - 1 - t, EXPERTS]),
                                         start=False, stop=False)
                    nc.tensor.matmul(pR, ones[:, :], chosen_all[:, :].unsqueeze(1).to_broadcast([P, QUAD, EXPERTS]),
                                     start=False, stop=True).then_inc(c_rank, 1)
                if has(s, 1):
                    q = s - 1
                    pe.wait_ge(a_qf, q + 1)
                    pe.wait_ge(b_mask, q + 1)
                    wait(pe, b_att, q)
                    wait(pe, c_x1, q)
                    for t in range(QUAD):
                        i = nc.tensor.matmul(pN[:, t, 0:RK], QF[:, par1, t * P:(t + 1) * P], KV[:, t // 2, :],
                                             start=True, stop=True)
                    i.then_inc(b_num, 1)
                if has(s, 0):
                    wait(pe, a_kf, s)
                    wait(pe, a_v, s)
                    for t in range(QUAD):
                        i = nc.tensor.matmul(pKVN[:, t, :], XNT[:, par, t * P:(t + 1) * P], WA[:, W_KV:W_KV + 2 * D],
                                             start=True, stop=True)
                    i.then_inc(a_kv, 1)
                if has(s, 2):
                    q = s - 2
                    pe.wait_ge(c_z, q + 1)
                    wait(pe, c_slot, q)
                    for t in range(QUAD):
                        i = nc.tensor.transpose(pZ[:, t * P:(t + 1) * P], Z[:, par, t, 0, 0:D], ident)
                    i.then_inc(c_T, 1)
                if has(s, 1):
                    q = s - 1
                    pe.wait_ge(b_att, q + 1)
                    for t in range(QUAD):
                        i = nc.tensor.transpose(pAT[:, t * P:(t + 1) * P], att[:, t, :], ident)
                    i.then_inc(b_T, 1)
                if has(s, 2):
                    q = s - 2
                    pe.wait_ge(c_zT, q + 1)
                    for t in range(QUAD):
                        i = nc.tensor.matmul(pL[:, t, :], zT[:, t * P:(t + 1) * P], WA[:, W_R:W_R + EXPERTS],
                                             start=True, stop=True)
                    i.then_inc(c_lg, 1)
                if has(s, 1):
                    q = s - 1
                    pe.wait_ge(b_aT, q + 1)
                    for t in range(QUAD):
                        i = nc.tensor.matmul(pO[:, t * P:(t + 1) * P], attT[:, t * P:(t + 1) * P], WA[:, W_O:W_O + D],
                                             start=True, stop=True)
                    i.then_inc(b_wo, 1)
                if has(s, -1):
                    tokens_t(s + 1, par1)

            nc.tensor.matmul(pQ[:, 0:D], ones_row[0:1, :], bo_row[0:1, :], start=True, stop=True).then_inc(s_bo_all, 1)
            pe.wait_ge(s_tri, 1)
            pe.wait_ge(s_bo_all, 2)
            tokens_t(0, 0)
            steps(pe, step)

            def rows_t(n, it, j):
                pe.wait_ge(xs[j], it * 16 + 16)
                wait(pe, s_xT, n)
                nc.tensor.transpose(pX, XS[:, j, 0:D], ident).then_inc(s_Tx, 1)

            def gate_up(n, j, e):
                pe.wait_ge(s_xT, n + 1)
                wait(pe, s_h, n - 1)
                nc.tensor.matmul(pGU[j % 2][:, 0:2 * EXP_DIM], xT[:, j % 2, :],
                                 WF[:, bass.ds(e * (2 * EXP_DIM) + F_GU, 2 * EXP_DIM)], start=True, stop=True).then_inc(s_gu, 1)

            def hidden_t(n, j):
                pe.wait_ge(s_h, n + 1)
                wait(pe, s_hT, n)
                nc.tensor.transpose(pHT, h[:, j % 2, :], ident).then_inc(s_Th, 1)

            def down(n, j, e):
                pe.wait_ge(s_hT, n + 1)
                wait(pe, s_y, n)
                nc.tensor.matmul(pY, hT[:, j % 2, :], WF[:, bass.ds(e * D + F_DN, D)], start=True, stop=True).then_inc(s_D, 1)

            def shared_gu(i):
                wait(pe, h_h, i)
                zt = ZT[:, bass.ds(i * HALF, HALF)]
                for f in range(2):
                    nc.tensor.matmul(pSG[:, f * HALF:(f + 1) * HALF], WF[:, F_SG + f * P:F_SG + (f + 1) * P], zt, start=True, stop=True)
                    l = nc.tensor.matmul(pSU[:, f * HALF:(f + 1) * HALF], WF[:, F_SU + f * P:F_SU + (f + 1) * P], zt, start=True, stop=True)
                l.then_inc(h_gu, 1)

            def shared_d(i):
                pe.wait_ge(h_h, i + 1)
                wait(pe, h_add, i)
                for t in range(2):
                    for f in range(2):
                        l = nc.tensor.matmul(pSD[:, t * D:(t + 1) * D],
                                             sh_h[:, f * HALF + t * P:f * HALF + (t + 1) * P],
                                             WF[:, F_SD + f * D:F_SD + (f + 1) * D], start=(f == 0), stop=(f == 1))
                l.then_inc(h_d, 1)

            def body(it, first):
                e = values(pe, table_e, it * BODY, BODY + LEAD, EXPERTS - 1)
                for j in range(BODY):
                    n = it * BODY + j
                    if j == 1:
                        shared_gu(it + AHEAD)
                    if j == 4:
                        shared_d(it + AHEAD)
                    rows_t(n, it, j)
                    if not (first and j < 1):
                        gate_up(n - 1, (j - 1) % BODY, e[j - 1 + LEAD])
                    if not (first and j < 2):
                        hidden_t(n - 2, (j - 2) % BODY)
                    if not (first and j < 3):
                        down(n - 3, (j - 3) % BODY, e[j - 3 + LEAD])

            pe.wait_ge(c_cha, NQ)
            pe.wait_ge(c_slot, NQ)
            nc.tensor.matmul(pZ[0:EXPERTS, 0:P], chosen_all[:, :], ones[:, :], start=True, stop=True)
            nc.tensor.matmul(pZ[0:1, 256:256 + EXPERTS], ones[:, 0:1], chosen_all[:, :], start=True, stop=True).then_inc(t_cnt, 1)
            pe.wait_ge(s_wf, 16)
            pe.wait_ge(c_zT2, NQ)
            shared_gu(0)
            pe.wait_ge(t_nb, 1)
            pe.wait_ge(t_pad, 2)
            nc.tensor.matmul(pZ[:, 0:2 * EXPERTS], nb[:, :], CN[0:EXPERTS, C_CUM:C_CUM + 2 * EXPERTS],
                             start=True, stop=True).then_inc(t_cum, 1)
            shared_gu(1)
            pe.wait_ge(t_tab, 1)
            for a in range(2):
                i = nc.tensor.matmul(pZ[0:1, 128 + a * P:128 + (a + 1) * P], table_f[:, a:a + 1], ident, start=True, stop=True)
            i.then_inc(t_row, 1)

            shared_d(0)
            with pe.Fori(1, AHEAD - 1) as i:
                shared_gu(i + 1)
                shared_d(i)
            shared_d(AHEAD - 1)
            pe.wait_ge(t_table, 2)
            body(0, True)
            with pe.Fori(1, TURNS) as it:
                body(it, False)
            e = values(pe, table_e, BLOCKS, LEAD, EXPERTS - 1)
            gate_up(BLOCKS - 1, BODY - 1, e[LEAD - 1])
            hidden_t(BLOCKS - 2, BODY - 2)
            down(BLOCKS - 3, BODY - 3, e[LEAD - 3])
            hidden_t(BLOCKS - 1, BODY - 1)
            down(BLOCKS - 2, BODY - 2, e[LEAD - 2])
            down(BLOCKS - 1, BODY - 1, e[LEAD - 1])

            shared_gu(AFTER)
            with pe.Fori(AFTER, HALVES - 1) as i:
                shared_gu(i + 1)
                shared_d(i)
            shared_d(HALVES - 1)


def kernel(L0_attn_x, L0_attn_wq, L0_attn_wk, L0_attn_wv, L0_attn_wo, L0_attn_bo, L0_ffn_router_w,
           L0_ffn_gate_up_w, L0_ffn_down_w, L0_ffn_shared_gate_w, L0_ffn_shared_up_w, L0_ffn_shared_down_w):
    import numpy as np
    import concourse.bacc as bacc
    from concourse.bass_utils import run_bass_kernel_spmd

    f32 = np.float32
    t = lambda a: np.asarray(a).T
    w_att = np.ascontiguousarray(np.concatenate(
        [t(L0_attn_wq), t(L0_attn_wk), t(L0_attn_wv), t(L0_attn_wo), t(L0_ffn_router_w)], axis=1))
    gate_up = np.asarray(L0_ffn_gate_up_w).transpose(1, 0, 2).reshape(D, -1)
    down = np.asarray(L0_ffn_down_w).transpose(1, 0, 2).reshape(EXP_DIM, -1)
    s_down = t(L0_ffn_shared_down_w).reshape(SHARED // P, P, D).transpose(1, 0, 2).reshape(P, -1)
    w_ffn = np.ascontiguousarray(np.concatenate(
        [gate_up, down, t(L0_ffn_shared_gate_w), t(L0_ffn_shared_up_w), s_down], axis=1))
    i, c = np.arange(P)[:, None], np.arange(P)[None, :]
    e = np.arange(EXPERTS)[None, :]
    consts = np.zeros((P, C_ALL), f32)
    consts[:, C_IDENT:C_IDENT + P] = i == c
    consts[:, C_TRI:C_TRI + P] = i < c
    consts[:, C_MASK:C_MASK + D] = i // HD == c // HD
    consts[:, C_MASK + D:C_MASK + RK] = i // HD == e
    consts[:, C_IOTA:C_IOTA + EXPERTS] = e
    consts[:, C_BASE:C_BASE + EXPERTS] = e * REGION
    consts[:, C_SLOT:C_SLOT + 1] = i
    consts[0:EXPERTS, C_CUM:C_CUM + EXPERTS] = i[:EXPERTS] <= e
    consts[0:EXPERTS, C_CUM + EXPERTS:C_ALL] = i[:EXPERTS] == e
    q, b, j, k = np.meshgrid(np.arange(NQ), np.arange(SPQ), np.arange(2), np.arange(TOP_K), indexing="ij")
    tokid = (k * TOKENS + q * QTOK + b * SEQ + j).reshape(1, -1) + 2 * i
    arrays = {
        "x": np.ascontiguousarray(np.asarray(L0_attn_x).reshape(TOKENS, D)),
        "w_att": w_att,
        "bo": np.ascontiguousarray(np.asarray(L0_attn_bo).reshape(1, D)),
        "w_ffn": w_ffn,
        "consts": consts,
        "tokid": tokid.astype(np.uint32),
    }
    nc = bacc.Bacc("TRN2", target_bir_lowering=False, num_devices=1)
    args = [nc.dram_tensor(n, a.shape, mybir.dt.from_np(a.dtype), kind="ExternalInput").ap() for n, a in arrays.items()]
    out = nc.dram_tensor("out", (TOKENS, D), mybir.dt.float32, kind="ExternalOutput").ap()
    preln_block(nc, *args, out)
    r = run_bass_kernel_spmd(nc, [arrays], core_ids=[0])
    return r.results[0]["out"].reshape(BATCHES, SEQ, D)
```

```python
import concourse.bass as bass
from concourse import mybir
from contextlib import ExitStack

P = 128
D = 128
HEADS = 16
HD = D // HEADS
BATCHES, SEQ = 16, 256
TOKENS = BATCHES * SEQ
EXPERTS, TOP_K = 16, 2
EXP_DIM = 128
SHARED = 256
LN_EPS, ATT_EPS = 1e-5, 1e-6

QUAD = 4
QTOK = QUAD * P
NQ = TOKENS // QTOK
SPQ = QTOK // SEQ
RK = D + HEADS
FULL = 4
PAIRS_OF_STEPS = (NQ - 1 - FULL) // 2

REGION = TOKENS + P
REGION_BLOCKS = REGION // P
ROW = D + 2
SKIP = 1 << 20
PAIRS = TOP_K * TOKENS
MAX_BLOCKS = PAIRS // P + EXPERTS - 1
BODY = 16
TURNS = -(-MAX_BLOCKS // BODY)
BLOCKS = TURNS * BODY
HALF = 2 * P
HALVES = TOKENS // HALF
AHEAD = 5
AFTER = AHEAD + TURNS - 1
ACT_PADS = 6
LEAD = 4

C_IDENT, C_TRI, C_MASK = 0, P, 2 * P
C_IOTA = C_MASK + RK
C_BASE = C_IOTA + EXPERTS
C_SLOT = C_BASE + EXPERTS
C_CUM = C_SLOT + 1
C_ALL = C_CUM + 2 * EXPERTS
W_Q, W_KV, W_O, W_R = 0, D, 3 * D, 4 * D
W_ALL = 4 * D + EXPERTS
F_EXP = 2 * EXP_DIM + D
F_SG = EXPERTS * F_EXP
F_SU = F_SG + SHARED
F_SD = F_SU + SHARED
F_ALL = F_SD + SHARED // P * D


def preln_block(nc, x, w_att, bo, w_ffn, consts, tokid, out):
    assert BODY % 2 == 0 and AHEAD % 2 == 1 and P == D == EXP_DIM
    F32, BF16 = mybir.dt.float32, mybir.dt.bfloat16
    U32, I32 = mybir.dt.uint32, mybir.dt.int32
    ALU, ACT, AX = mybir.AluOpType, mybir.ActivationFunctionType, mybir.AxisListType

    x_v = x.rearrange("(q b p j) c -> q p b (j c)", b=SPQ, p=P, j=2)
    out_v = out.rearrange("(q b p j) c -> q p b (j c)", b=SPQ, p=P, j=2)

    with ExitStack() as ctx:
        def sb(name, shape, dt=F32):
            return ctx.enter_context(nc.sbuf_tensor(name, shape, dt))

        def pb(name, shape):
            return ctx.enter_context(nc.psum_tensor(name, shape, F32))

        def sem(name):
            return ctx.enter_context(nc.semaphore(name))

        routed = nc.dram_tensor("routed", ((EXPERTS + 1) * REGION, ROW), F32, kind="Internal").ap()
        results = nc.dram_tensor("results", (PAIRS, D), F32, kind="Internal").ap()
        res_v = results.rearrange("(k q b p j) c -> k q p b (j c)", k=TOP_K, b=SPQ, p=P, j=2)

        X = sb("X", [P, NQ * QTOK])
        X1 = sb("X1", [P, NQ * QTOK])
        ZT = sb("ZT", [P, NQ * QTOK])
        WA = sb("WA", [P, W_ALL])
        WF = sb("WF", [P, F_ALL])
        CN = sb("CN", [P, C_ALL])
        TOK = sb("TOK", [P, NQ * QUAD * TOP_K], U32)
        bo_row = sb("bo_row", [1, D])
        bo_all = sb("bo_all", [P, D])
        ones_row = sb("ones_row", [1, P])
        ones = sb("ones", [P, P], BF16)
        tri = sb("tri", [P, P], BF16)
        eps = sb("eps", [P, 1])
        ident = CN[:, C_IDENT:C_IDENT + P]

        a_stat = sb("a_stat", [P, NQ * QUAD, 6])
        a_mv = sb("a_mv", [P, NQ * QUAD, 2])
        a_rs = sb("a_rs", [P, 6, NQ * QUAD])
        XN = sb("XN", [P, 2, QUAD, D])
        XNT = sb("XNT", [P, 2, QTOK])
        rq = sb("rq", [P, QTOK])
        eq = sb("eq", [P, QTOK])
        rk = sb("rk", [P, QUAD, D])
        ek = sb("ek", [P, QUAD, D])
        QF = sb("QF", [P, 2, QTOK])
        KF = sb("KF", [P, 2, QUAD, D])
        V = sb("V", [P, 2, QUAD, D + 4])
        KV = sb("KV", [P, SPQ, RK])
        den = sb("den", [P, QUAD, HEADS])
        rden = sb("rden", [P, QUAD, HEADS])
        att = sb("att", [P, QUAD, D])
        attT = sb("attT", [P, QTOK])
        c_stat = sb("c_stat", [P, QUAD, 6])
        c_mv = sb("c_mv", [P, QUAD, 2])
        c_rs = sb("c_rs", [P, 6, QUAD])
        Z = sb("Z", [P, 2, QUAD, TOP_K, ROW])
        zT = sb("zT", [P, QTOK])
        top = sb("top", [P, QUAD, 8])
        top_i = sb("top_i", [P, QUAD, 8], U32)
        onehot = sb("onehot", [P, QUAD, TOP_K, EXPERTS])
        chosen = sb("chosen", [P, QUAD, EXPERTS], BF16)
        chosen_q = sb("chosen_q", [P, EXPERTS], BF16)
        chosen_all = sb("chosen_all", [P, EXPERTS], BF16)
        slot = sb("slot", [P, QUAD, EXPERTS])
        slot_k = sb("slot_k", [P, QUAD, TOP_K, EXPERTS])
        ROWS = sb("ROWS", [P, 2, QUAD, TOP_K], U32)
        gate_e = sb("gate_e", [P, QUAD, TOP_K])
        gate_1 = sb("gate_1", [P, QUAD, TOP_K])
        pad = sb("pad", [P, ROW])
        pad_at = sb("pad_at", [1, EXPERTS], I32)
        nb_a = sb("nb_a", [EXPERTS, P], I32)
        nb_b = sb("nb_b", [EXPERTS, P], I32)
        nb = sb("nb", [EXPERTS, P])
        before = sb("before", [P, EXPERTS])
        before_nb = sb("before_nb", [P, EXPERTS])
        blk = sb("blk", [P, 3])
        table_f = sb("table_f", [P, 2])
        table_b = sb("table_b", [1, LEAD + P], I32)
        table_e = sb("table_e", [1, LEAD + P], I32)
        XS = sb("XS", [P, BODY, ROW])
        Y = sb("Y", [P, BODY, D])
        xhT = sb("xhT", [P, 2, 2, P])
        sg = sb("sg", [P, 2, EXP_DIM])
        h = sb("h", [P, 2, EXP_DIM])
        sh_s = sb("sh_s", [P, 2 * HALF])
        sh_h = sb("sh_h", [P, 2 * HALF])
        YL = sb("YL", [P, NQ, TOP_K, QTOK])
        ysum = YL[:, :, 0, :]

        pT = pb("pT", [P, 512])
        pQ = pb("pQ", [P, 512])
        pKVN = pb("pKVN", [P, QUAD, 256])
        pKV = pb("pKV", [P, 2, 256])
        pN = pb("pN", [P, QUAD, 256])
        pZ = pb("pZ", [P, 512])
        pO = pN[:, 0:2, :].rearrange("p a c -> p (a c)")
        pAT = pKV[:, :, :].rearrange("p a c -> p (a c)")
        pL = pZ[:, 0:QUAD * EXPERTS].rearrange("p (t e) -> p t e", e=EXPERTS)
        pR = pZ[:, 128:128 + QUAD * EXPERTS].rearrange("p (t e) -> p t e", e=EXPERTS)
        pXH = pT[:, 0:2 * P].rearrange("p (a c) -> p a c", a=2)
        pGU = [pQ, pZ]
        pY = pKVN[:, 0, 0:D]
        pSG = [pKVN[:, 2:4, :].rearrange("p a c -> p (a c)"), pQ]
        pSU = [pN[:, 0:2, :].rearrange("p a c -> p (a c)"), pN[:, 2:4, :].rearrange("p a c -> p (a c)")]
        pSD = pAT[:, 0:2 * D]

        s_cn, s_tok, s_wa, s_wf = sem("s_cn"), sem("s_tok"), sem("s_wa"), sem("s_wf")
        waited = sem("waited")
        s_x = sem("s_x")
        s_ones, s_tri, s_bo, s_bo_all = sem("s_ones"), sem("s_tri"), sem("s_bo"), sem("s_bo_all")
        s_xb = sem("s_xb")
        a_stats, a_aggr, a_rstd, a_norm = sem("a_stats"), sem("a_aggr"), sem("a_rstd"), sem("a_norm")
        a_ln, a_y, a_n1, a_n2 = sem("a_ln"), sem("a_y"), sem("a_n1"), sem("a_n2")
        a_shift = sem("a_shift")
        c_ln, c_y, c_n1, c_n2 = sem("c_ln"), sem("c_y"), sem("c_n1"), sem("c_n2")
        a_T, a_xT, a_q, a_kv = sem("a_T"), sem("a_xT"), sem("a_q"), sem("a_kv")
        a_rk, a_ek, a_rq, a_eq, a_v = sem("a_rk"), sem("a_ek"), sem("a_rq"), sem("a_eq"), sem("a_v")
        a_kf, a_qf = sem("a_kf"), sem("a_qf")
        b_kv, b_mask, b_num = sem("b_kv"), sem("b_mask"), sem("b_num")
        b_den, b_rden, b_att = sem("b_den"), sem("b_rden"), sem("b_att")
        b_T, b_aT, b_wo = sem("b_T"), sem("b_aT"), sem("b_wo")
        c_x1, c_stats, c_aggr, c_rstd = sem("c_x1"), sem("c_stats"), sem("c_aggr"), sem("c_rstd")
        c_z, c_zdup, c_T, c_zT, c_zT2 = sem("c_z"), sem("c_zdup"), sem("c_T"), sem("c_zT"), sem("c_zT2")
        c_lg, c_top, c_idx = sem("c_lg"), sem("c_top"), sem("c_idx")
        c_oh, c_ch, c_rank, c_chq, c_cha = sem("c_oh"), sem("c_ch"), sem("c_rank"), sem("c_chq"), sem("c_cha")
        c_slot, c_slotk, c_rows = sem("c_slot"), sem("c_slotk"), sem("c_rows")
        c_ge, c_g1, c_pay = sem("c_ge"), sem("c_g1"), sem("c_pay")
        scat = [sem("scat0"), sem("scat1")]
        t_cnt, t_nba, t_nbb, t_nb, t_cum = sem("t_cnt"), sem("t_nba"), sem("t_nbb"), sem("t_nb"), sem("t_cum")
        t_v, t_tab, t_row, t_table, t_pad, t_pads = (sem("t_v"), sem("t_tab"), sem("t_row"),
                                                     sem("t_table"), sem("t_pad"), sem("t_pads"))
        xs = [sem(f"xs{j}") for j in range(BODY // 2)]
        ysc = [sem(f"ysc{j}") for j in range(BODY // 2)]
        s_T, s_xhT, s_gu, s_silu, s_h = sem("s_T"), sem("s_xhT"), sem("s_gu"), sem("s_silu"), sem("s_h")
        s_D, s_y = sem("s_D"), sem("s_y")
        h_gu, h_silu, h_h, h_d, h_add = sem("h_gu"), sem("h_silu"), sem("h_h"), sem("h_d"), sem("h_add")
        yl = [sem(f"yl{q}") for q in range(NQ)]
        c_sum, c_out, s_out = sem("c_sum"), sem("c_out"), sem("s_out")

        def wait(eng, semaphore, count):
            if not isinstance(count, int) or count > 0:
                eng.wait_ge(semaphore, count)

        def quad(t, q):
            return t[:, bass.ds(q * QTOK, QTOK)]

        def steps(eng, step):
            for s in range(FULL):
                step(s, s % 2)
            with eng.Fori(0, PAIRS_OF_STEPS) as it:
                for u in range(2):
                    step(it * 2 + (FULL + u), (FULL + u) % 2)
            for s in range(FULL + 2 * PAIRS_OF_STEPS, NQ + 3):
                step(s, s % 2)

        def unit(u):
            return range(u * QUAD, (u + 1) * QUAD) if u < 2 else range((2 * u - 2) * QUAD, 2 * u * QUAD)

        def final(s):
            return isinstance(s, int) and s == NQ + 1

        def stats(s):
            return isinstance(s, int) and 0 < 2 * s < NQ

        def wait_apart(eng, semaphore, count):
            eng.wait_ge(semaphore, count)
            eng.sem_inc(waited, 1)

        def has(s, lag):
            return not isinstance(s, int) or 0 <= s - lag < NQ

        def values(eng, row, start, count, most):
            return nc.values_load_multi_w_load_instructions(
                row[0:1, bass.ds(start, count)], engines=(eng.engine,), min_val=0, max_val=most,
                skip_runtime_bounds_check_because="the table is clamped where it is made")[1]

        def pads(eng, first, count):
            for at in values(eng, pad_at, first, count, EXPERTS * REGION - P):
                eng.dma_start(routed[bass.ds(at, P), :], pad[:, :]).then_inc(t_pads, 16)

        block = ctx.enter_context(nc.Block())

        @block.sync
        def _(sp):
            sp.dma_start(quad(X, 0).rearrange("p (b f) -> p b f", b=SPQ), x_v[0]).then_inc(s_x, 16)
            sp.dma_start(bo_row[0:1, :], bo).then_inc(s_bo, 16)
            sp.wait_ge(s_x, 16)
            with sp.Fori(1, NQ) as q:
                sp.dma_start(quad(X, q).rearrange("p (b f) -> p b f", b=SPQ),
                             x_v[bass.ds(q, 1)].rearrange("o p b f -> (o p) b f")).then_inc(s_x, 16)
                wait_apart(sp, s_x, q * 16 + 16)
            sp.dma_start(WF[:, :], w_ffn).then_inc(s_wf, 16)

            sp.wait_ge(t_pad, 2)
            pads(sp, 0, EXPERTS - ACT_PADS)
            sp.dma_start(routed[EXPERTS * REGION:EXPERTS * REGION + P, :], pad[:, :]).then_inc(t_pads, 16)
            sp.wait_ge(t_pads, 16 * (EXPERTS + 1))
            for s_ in scat:
                sp.wait_ge(s_, 16 * QUAD * TOP_K * NQ // 2)
            sp.wait_ge(t_table, 2)

            def load(it):
                at = values(sp, table_b, it * BODY + LEAD, BODY, EXPERTS * REGION_BLOCKS)
                for j in range(BODY):
                    if j % 2 == 0:
                        wait(sp, ysc[j // 2], it * 32)
                    sp.dma_start(XS[:, j, :], routed[bass.ds(at[j] * P, P), :]).then_inc(xs[j // 2], 16)

            load(0)
            with sp.Fori(1, TURNS) as it:
                load(it)

            for s_ in ysc:
                sp.wait_ge(s_, 32 * TURNS)

            for q in range(NQ):
                for k in range(TOP_K):
                    sp.dma_start(YL[:, q, k, :].rearrange("p (b f) -> p b f", b=SPQ), res_v[k, q]).then_inc(yl[q], 16)
            with sp.Fori(0, NQ) as q:
                wait_apart(sp, c_out, q + 1)
                sp.dma_start(out_v[bass.ds(q, 1)].rearrange("o p b f -> (o p) b f"),
                             quad(X1, q).rearrange("p (b f) -> p b f", b=SPQ)).then_inc(s_out, 16)
            sp.wait_ge(s_out, 16 * NQ)

        @block.gpsimd
        def _(pool):
            pool.wait_ge(s_bo_all, 2)
            bo_q = bo_all[:, :].unsqueeze(1).to_broadcast([P, QUAD, D])
            with pool.Fori(0, NQ) as q:
                pool.wait_ge(s_x, q * 16 + 16)
                nc.gpsimd.tensor_tensor(quad(X1, q).rearrange("p (t c) -> p t c", t=QUAD),
                                        quad(X, q).rearrange("p (t c) -> p t c", t=QUAD),
                                        bo_q, ALU.add).then_inc(s_xb, 1)

            def dispatch(q, par):
                pool.wait_ge(c_rows, q + 1)
                pool.wait_ge(c_pay, q + 1)
                wait_apart(pool, c_zdup, q + 1)
                for t in range(QUAD):
                    for k in range(TOP_K):
                        nc.gpsimd.indirect_dma_start(
                            routed, bass.IndirectOffsetOnAxis(ap=ROWS[:, par, t, k:k + 1], axis=0),
                            Z[:, par, t, k, :], None).then_inc(scat[par], 16)

            with pool.Fori(0, NQ // 2) as it:
                for par in range(2):
                    dispatch(it * 2 + par, par)

            with pool.Fori(0, TURNS) as it:
                for j in range(BODY):
                    if j % 2 == 0:
                        wait_apart(pool, s_y, it * BODY + (j + 2))
                    nc.gpsimd.indirect_dma_start(
                        results, bass.IndirectOffsetOnAxis(ap=XS[:, j, D:D + 1].bitcast(U32), axis=0),
                        Y[:, j, :], None, bounds_check=PAIRS - 1, oob_is_err=False).then_inc(ysc[j // 2], 16)

            for q in range(NQ):
                pool.wait_ge(yl[q], 16 * TOP_K)
                nc.gpsimd.tensor_tensor(ysum[:, q, :], YL[:, q, 0, :], YL[:, q, 1, :], ALU.add).then_inc(c_sum, 1)

        @block.scalar
        def _(act):
            act.dma_start(CN[:, :], consts).then_inc(s_cn, 16)
            act.dma_start(WA[:, :], w_att).then_inc(s_wa, 16)
            act.dma_start(TOK[:, :], tokid).then_inc(s_tok, 16)

            def rstd(mv, rs, aggr, ln, y, q, tiles=range(QUAD)):
                t = slice(tiles.start, tiles.stop)
                act.wait_ge(aggr, q + 1)
                nc.scalar.activation(rs[:, 0, t], mv[:, t, 1], ACT.Ln, bias=eps[:, 0:1]).then_inc(ln, 1)
                act.wait_ge(ln, q + 1)
                nc.scalar.activation(rs[:, 1, t], rs[:, 0, t], ACT.Exp, scale=-0.5).then_inc(y, 1)

            act.preload_act_table_set("natural_log_exp_and_others")
            rstd(a_mv, a_rs, a_aggr, a_ln, a_y, 0, unit(0))

            def norm1(q, par):
                if isinstance(q, int):
                    act.wait_ge(a_shift, q + 1 if q < 2 else q // 2 + 2)
                wait(act, a_T, q - 1)
                for t in range(QUAD):
                    i = nc.scalar.activation(XN[:, par, t, :], X[:, bass.ds(q * QTOK + t * D, D)], ACT.Identity,
                                             bias=a_rs[:, 5, bass.ds(q * QUAD + t, 1)],
                                             scale=a_rs[:, 4, bass.ds(q * QUAD + t, 1)])
                i.then_inc(a_norm, 1)

            norm1(0, 0)
            rstd(a_mv, a_rs, a_aggr, a_ln, a_y, 1, unit(1))

            def tokens_t(q, par):
                act.wait_ge(a_T, q + 1)
                wait(act, a_kv, q - 1)
                nc.scalar.copy(XNT[:, par, :], pT[:, :]).then_inc(a_xT, 1)

            tokens_t(0, 0)
            norm1(1, 1)

            def step(s, par):
                this, att_, last, coming = has(s, 0), has(s, 1), has(s, 2), has(s, -1)
                if last:
                    rstd(c_mv, c_rs, c_aggr, c_ln, c_y, s - 2)
                if this:
                    act.wait_ge(a_q, s + 1)
                    nc.scalar.activation(rq[:, :], pQ[:, :], ACT.Relu, scale=-1.0).then_inc(a_rq, 1)
                    act.wait_ge(a_rq, s + 1)
                    wait(act, a_qf, s)
                    nc.scalar.activation(eq[:, :], rq[:, :], ACT.Exp, scale=-1.0).then_inc(a_eq, 1)
                if stats(s):
                    rstd(a_mv, a_rs, a_aggr, a_ln, a_y, s + 1, unit(s + 1))
                if this:
                    act.wait_ge(a_kv, s + 1)
                    nc.scalar.activation(rk[:, :, :], pKVN[:, :, 0:D], ACT.Relu, scale=-1.0).then_inc(a_rk, 1)
                if last:
                    q = s - 2
                    act.wait_ge(c_T, q + 1)
                    wait(act, c_lg, q)
                    nc.scalar.copy(zT[:, :], pZ[:, :]).then_inc(c_zT, 1)
                if this:
                    wait(act, b_kv, s - 1)
                    nc.scalar.copy(V[:, par, :, 0:D], pKVN[:, :, D:2 * D]).then_inc(a_v, 1)
                    act.wait_ge(a_rk, s + 1)
                    wait(act, a_kf, s)
                    nc.scalar.activation(ek[:, :, :], rk[:, :, :], ACT.Exp, scale=-1.0).then_inc(a_ek, 1)
                if att_:
                    q = s - 1
                    act.wait_ge(b_T, q + 1)
                    wait(act, b_wo, q)
                    nc.scalar.copy(attT[:, :], pAT).then_inc(b_aT, 1)
                if coming and not (isinstance(s, int) and s == 0):
                    norm1(s + 1, 1 - par)
                if last:
                    q = s - 2
                    act.wait_ge(c_top, q + 1)
                    wait(act, c_g1, q)
                    nc.scalar.activation(gate_e[:, :, :], top[:, :, 0:TOP_K], ACT.Exp, scale=-1.0).then_inc(c_ge, 1)
                    act.wait_ge(c_z, q + 1)
                    nc.scalar.copy(Z[:, par, :, 1, 0:D], Z[:, par, :, 0, 0:D]).then_inc(c_zdup, 1)
                if coming:
                    tokens_t(s + 1, 1 - par)
                if last:
                    q = s - 2
                    act.wait_ge(c_zT, q + 1)
                    nc.scalar.copy(quad(ZT, q), zT[:, :]).then_inc(c_zT2, 1)

            steps(act, step)

            def silu(n, j):
                act.wait_ge(s_gu, n + 1)
                wait(act, s_h, n - 1)
                nc.scalar.activation(sg[:, j % 2, :], pGU[j % 2][:, 0:EXP_DIM], ACT.Silu).then_inc(s_silu, 1)

            def scaled(n, j):
                act.wait_ge(s_D, n + 1)
                nc.scalar.activation(Y[:, j, :], pY, ACT.Copy, scale=XS[:, j, D + 1:D + 2]).then_inc(s_y, 1)

            def shared(i, pair=0):
                act.wait_ge(h_gu, i + 1)
                wait(act, h_h, i)
                nc.scalar.activation(sh_s[:, :], pSG[pair][:, :], ACT.Silu).then_inc(h_silu, 1)

            shared(0)
            act.wait_ge(t_pad, 2)
            for i in range(1, AHEAD):
                if i <= ACT_PADS // 2:
                    pads(act, EXPERTS - ACT_PADS + 2 * (i - 1), 2)
                shared(i, i % 2)

            def body(it, first):
                for j in range(BODY):
                    n = it * BODY + j
                    if not first and j == 5:
                        shared(it + (AHEAD - 1))
                    if not (first and j < 1):
                        silu(n - 1, (j - 1) % BODY)
                    if not (first and j < 4):
                        scaled(n - 4, (j - 4) % BODY)

            body(0, True)
            with act.Fori(1, TURNS) as it:
                body(it, False)
            silu(BLOCKS - 1, BODY - 1)
            for k in range(4, 0, -1):
                scaled(BLOCKS - k, BODY - k)

            for i in range(AFTER, HALVES):
                shared(i, i % 2)

        @block.vector
        def _(dve):
            nc.vector.memset(ones_row[:, :], 1.0)
            nc.vector.memset(ones[:, :], 1.0)
            nc.vector.memset(chosen_all[:, :], 0.0)
            nc.vector.memset(table_e[0:1, 0:LEAD], 0).then_inc(t_table, 1)
            nc.vector.memset(eps[:, :], LN_EPS)
            nc.vector.memset(pad[:, :], 0.0).then_inc(t_pad, 1)
            nc.vector.memset(V[:, :, :, D:D + 1], 1.0).then_inc(s_ones, 1)
            dve.wait_ge(t_pad, 1)
            nc.vector.memset(pad[:, D:D + 1].bitcast(U32), SKIP).then_inc(s_ones, 1)

            def bn_stats(src, at, stat, stats, tiles=range(QUAD)):
                for t in tiles:
                    i = nc.vector.bn_stats(stat[:, t, :], src[:, bass.ds(at + t * D, D)])
                i.then_inc(stats, 1)

            def bn_aggr(stat, mv, stats, aggr, q, tiles=range(QUAD)):
                wait_apart(dve, stats, q + 1)
                for t in tiles:
                    i = nc.vector.bn_aggr(mv[:, t, :], stat[:, t, :])
                i.then_inc(aggr, 1)

            def newton1(mv, rs, y, n1, q, tiles=range(QUAD)):
                t = slice(tiles.start, tiles.stop)
                dve.wait_ge(y, q + 1)
                nc.vector.scalar_tensor_tensor(rs[:, 2, t], mv[:, t, 1], LN_EPS, rs[:, 1, t], ALU.add, ALU.mult).then_inc(n1, 1)

            def newton2(rs, n1, n2, q, tiles=range(QUAD)):
                t = slice(tiles.start, tiles.stop)
                dve.wait_ge(n1, q + 1)
                nc.vector.scalar_tensor_tensor(rs[:, 3, t], rs[:, 2, t], -0.5, rs[:, 1, t], ALU.mult, ALU.mult).then_inc(n2, 1)

            def newton3(rs, n2, rstd, q, tiles=range(QUAD)):
                t = slice(tiles.start, tiles.stop)
                dve.wait_ge(n2, q + 1)
                nc.vector.scalar_tensor_tensor(rs[:, 4, t], rs[:, 3, t], 1.5, rs[:, 1, t], ALU.add, ALU.mult).then_inc(rstd, 1)

            def shift1(u):
                t = slice(unit(u).start, unit(u).stop)
                dve.wait_ge(a_rstd, u + 1)
                nc.vector.scalar_tensor_tensor(a_rs[:, 5, t], a_mv[:, t, 0], -1.0, a_rs[:, 4, t], ALU.mult, ALU.mult).then_inc(a_shift, 1)

            def residual(q):
                dve.wait_ge(b_wo, q + 1)
                dve.wait_ge(s_xb, q + 1)
                nc.vector.tensor_tensor(quad(X1, q), pO, quad(X1, q), ALU.add).then_inc(c_x1, 1)

            def norm2(q, par, dispatched):
                dve.wait_ge(c_rstd, q + 1)
                wait(dve, scat[par], dispatched)
                for t in range(QUAD):
                    i = nc.vector.tensor_scalar(Z[:, par, t, 0, 0:D], X1[:, bass.ds(q * QTOK + t * D, D)],
                                                c_mv[:, t, 0:1], c_rs[:, 4, t:t + 1], ALU.subtract, ALU.mult)
                i.then_inc(c_z, 1)

            def mask(q):
                dve.wait_ge(b_kv, q + 1)
                wait(dve, b_num, q)
                nc.vector.tensor_tensor(
                    KV[:, :, 0:D], pKV[:, :, 0:D],
                    CN[:, C_MASK:C_MASK + D].unsqueeze(1).to_broadcast([P, SPQ, D]), ALU.mult)
                nc.vector.tensor_tensor(
                    KV[:, :, D:RK], pKV[:, :, D:D + 1].to_broadcast([P, SPQ, HEADS]),
                    CN[:, C_MASK + D:C_MASK + RK].unsqueeze(1).to_broadcast([P, SPQ, HEADS]),
                    ALU.mult).then_inc(b_mask, 1)

            def attend1(q):
                dve.wait_ge(b_num, q + 1)
                nc.vector.tensor_scalar(den[:, :, :], pN[:, :, D:RK], ATT_EPS, None, ALU.add).then_inc(b_den, 1)
                dve.wait_ge(b_den, q + 1)
                nc.vector.reciprocal(rden[:, :, :], den[:, :, :]).then_inc(b_rden, 1)

            def attend2(q):
                dve.wait_ge(b_rden, q + 1)
                wait(dve, b_T, q)
                nc.vector.tensor_tensor(
                    att[:, :, :].rearrange("p t (h d) -> p t h d", d=HD),
                    pN[:, :, 0:D].rearrange("p t (h d) -> p t h d", d=HD),
                    rden[:, :, :].unsqueeze(3).to_broadcast([P, QUAD, HEADS, HD]), ALU.mult).then_inc(b_att, 1)

            def features_q(q, par):
                dve.wait_ge(a_eq, q + 1)
                wait(dve, b_num, q - 1)
                nc.vector.scalar_tensor_tensor(QF[:, par, :], pQ[:, :], 1.0, eq[:, :], ALU.add, ALU.max).then_inc(a_qf, 1)

            def features_k(q, par):
                dve.wait_ge(a_ek, q + 1)
                wait(dve, b_kv, q - 1)
                nc.vector.scalar_tensor_tensor(KF[:, par, :, :], pKVN[:, :, 0:D], 1.0, ek[:, :, :],
                                               ALU.add, ALU.max).then_inc(a_kf, 1)

            def route(q, par):
                wait_apart(dve, c_lg, q + 1)
                for t in range(QUAD):
                    i = nc.vector.max(top[:, t, :], pL[:, t, :])
                i.then_inc(c_top, 1)
                nc.vector.tensor_copy(Z[:, par, :, :, D].bitcast(U32),
                                      TOK[:, bass.ds(q * QUAD * TOP_K, QUAD * TOP_K)].rearrange("p (t k) -> p t k", k=TOP_K))
                wait_apart(dve, c_top, q + 1)
                for t in range(QUAD):
                    i = nc.vector.max_index(top_i[:, t, :], top[:, t, :], pL[:, t, :])
                i.then_inc(c_idx, 1)
                dve.wait_ge(c_idx, q + 1)
                nc.vector.tensor_tensor(
                    onehot[:, :, :, :],
                    CN[:, C_IOTA:C_IOTA + EXPERTS].unsqueeze(1).unsqueeze(1).to_broadcast([P, QUAD, TOP_K, EXPERTS]),
                    top_i[:, :, 0:TOP_K].unsqueeze(3).to_broadcast([P, QUAD, TOP_K, EXPERTS]),
                    ALU.is_equal).then_inc(c_oh, 1)
                dve.wait_ge(c_oh, q + 1)
                nc.vector.tensor_tensor(chosen[:, :, :], onehot[:, :, 0, :], onehot[:, :, 1, :], ALU.add).then_inc(c_ch, 1)
                dve.wait_ge(c_ge, q + 1)
                nc.vector.tensor_scalar(gate_1[:, :, :], gate_e[:, :, :], 1.0, None, ALU.add).then_inc(c_g1, 1)
                dve.wait_ge(c_ch, q + 1)
                with nc.allow_low_precision("counts up to 32 are exact in bfloat16"):
                    nc.vector.tensor_reduce(chosen_q[:, :], chosen[:, :, :].rearrange("p t e -> p e t"), AX.X, ALU.add).then_inc(c_chq, 1)
                dve.wait_ge(c_g1, q + 1)
                nc.vector.reciprocal(Z[:, par, :, :, D + 1], gate_1[:, :, :]).then_inc(c_pay, 1)

            def rows1(q):
                dve.wait_ge(c_rank, q + 1)
                nc.vector.tensor_tensor(
                    slot[:, :, :], pR,
                    CN[:, C_BASE:C_BASE + EXPERTS].unsqueeze(1).to_broadcast([P, QUAD, EXPERTS]), ALU.add).then_inc(c_slot, 1)
                dve.wait_ge(c_chq, q + 1)
                nc.vector.tensor_tensor(chosen_all[:, :], chosen_all[:, :], chosen_q[:, :], ALU.add).then_inc(c_cha, 1)

            def rows2(q):
                dve.wait_ge(c_slot, q + 1)
                nc.vector.tensor_tensor(slot_k[:, :, :, :], onehot[:, :, :, :],
                                        slot[:, :, :].unsqueeze(2).to_broadcast([P, QUAD, TOP_K, EXPERTS]),
                                        ALU.mult).then_inc(c_slotk, 1)

            def rows3(q, par):
                dve.wait_ge(c_slotk, q + 1)
                with nc.allow_low_precision("row numbers are whole and below 2 ** 24"):
                    nc.vector.tensor_reduce(ROWS[:, par, :, :], slot_k[:, :, :, :], AX.X, ALU.add).then_inc(c_rows, 1)

            def step(s, par):
                this, att_, last, tail, coming = has(s, 0), has(s, 1), has(s, 2), has(s, 3), has(s, -1)
                if last:
                    residual(s - 2)
                    wait_apart(dve, c_x1, s - 1)
                    bn_stats(X1, (s - 2) * QTOK, c_stat, c_stats)
                    bn_aggr(c_stat, c_mv, c_stats, c_aggr, s - 2)
                if att_:
                    mask(s - 1)
                if stats(s):
                    wait_apart(dve, s_x, unit(s + 1).stop // QUAD * 16)
                    bn_stats(X, 0, a_stat, a_stats, unit(s + 1))
                if last:
                    newton1(c_mv, c_rs, c_y, c_n1, s - 2)
                if tail:
                    rows1(s - 3)
                if last:
                    newton2(c_rs, c_n1, c_n2, s - 2)
                if tail:
                    rows2(s - 3)
                if last:
                    newton3(c_rs, c_n2, c_rstd, s - 2)
                if tail:
                    rows3(s - 3, 1 - par)
                if last:
                    q = s - 2
                    if isinstance(q, int):
                        dispatched = (q // 2) * 128
                    else:
                        dispatched = (q - 1) * 64 if par == 1 else q * 64
                    norm2(q, par, dispatched)
                if stats(s):
                    bn_aggr(a_stat, a_mv, a_stats, a_aggr, s + 1, unit(s + 1))
                if this:
                    features_q(s, par)
                if stats(s):
                    newton1(a_mv, a_rs, a_y, a_n1, s + 1, unit(s + 1))
                if att_:
                    attend1(s - 1)
                if stats(s):
                    newton2(a_rs, a_n1, a_n2, s + 1, unit(s + 1))
                if att_:
                    attend2(s - 1)
                if stats(s):
                    newton3(a_rs, a_n2, a_rstd, s + 1, unit(s + 1))
                    shift1(s + 1)
                if this:
                    features_k(s, par)
                if last:
                    route(s - 2, par)

            def statistics(u):
                wait_apart(dve, s_x, unit(u).stop // QUAD * 16)
                bn_stats(X, 0, a_stat, a_stats, unit(u))
                bn_aggr(a_stat, a_mv, a_stats, a_aggr, u, unit(u))

            statistics(0)
            dve.wait_ge(s_cn, 16)
            nc.vector.tensor_copy(tri[:, :], CN[:, C_TRI:C_TRI + P]).then_inc(s_tri, 1)
            for u in range(2):
                newton1(a_mv, a_rs, a_y, a_n1, u, unit(u))
                newton2(a_rs, a_n1, a_n2, u, unit(u))
                newton3(a_rs, a_n2, a_rstd, u, unit(u))
                shift1(u)
                if u == 0:
                    statistics(1)
            dve.wait_ge(s_bo_all, 1)
            nc.vector.tensor_copy(bo_all[:, :], pQ[:, 0:D]).then_inc(s_bo_all, 1)
            dve.wait_ge(s_tok, 16)
            steps(dve, step)

            def transposed(n, j, rows=True, hid=True):
                a, b = (0 if rows else 1), (2 if hid else 1)
                dve.wait_ge(s_T, n + 1)
                wait(dve, s_D, n - 4)
                nc.vector.tensor_copy(xhT[:, j % 2, a:b, :], pXH[:, a:b, :]).then_inc(s_xhT, 1)

            def hidden(n, j):
                dve.wait_ge(s_silu, n + 1)
                nc.vector.tensor_tensor(h[:, j % 2, :], pGU[j % 2][:, EXP_DIM:2 * EXP_DIM], sg[:, j % 2, :],
                                        ALU.mult).then_inc(s_h, 1)

            def shared_h(i, pair=0):
                dve.wait_ge(h_silu, i + 1)
                wait(dve, h_d, i)
                nc.vector.tensor_tensor(sh_h[:, :], pSU[pair], sh_s[:, :], ALU.mult).then_inc(h_h, 1)

            def shared_add(i):
                dve.wait_ge(h_d, i + 1)
                x1 = X1[:, bass.ds(i * HALF, HALF)]
                nc.vector.tensor_tensor(x1, pSD, x1, ALU.add).then_inc(h_add, 1)

            dve.wait_ge(t_cnt, 1)
            cnt = pZ[0:EXPERTS, 0:P]
            nc.vector.tensor_scalar(nb_a[:, :], cnt, float(P - 1), None, ALU.add).then_inc(t_nba, 1)
            nc.vector.tensor_tensor(pad_at[0:1, :], pZ[0:1, 256:256 + EXPERTS], CN[0:1, C_BASE:C_BASE + EXPERTS],
                                    ALU.add).then_inc(t_pad, 1)
            dve.wait_ge(t_nba, 1)
            nc.vector.tensor_single_scalar(nb_b[:, :], nb_a[:, :], 7, ALU.arith_shift_right).then_inc(t_nbb, 1)
            dve.wait_ge(t_nbb, 1)
            nc.vector.tensor_copy(nb[:, :], nb_b[:, :]).then_inc(t_nb, 1)
            shared_h(0)
            dve.wait_ge(t_cum, 1)
            cum = pZ[:, 0:EXPERTS]
            nbs = pZ[:, EXPERTS:2 * EXPERTS]
            slot_id = CN[:, C_SLOT:C_SLOT + 1]
            nc.vector.tensor_scalar(before[:, :], cum, slot_id, None, ALU.is_le).then_inc(t_v, 1)
            dve.wait_ge(t_v, 1)
            nc.vector.tensor_tensor(before_nb[:, :], before[:, :], nbs, ALU.mult).then_inc(t_v, 1)
            nc.vector.tensor_reduce(blk[:, 0:1], before[:, :], AX.X, ALU.add).then_inc(t_v, 1)
            dve.wait_ge(t_v, 3)
            nc.vector.tensor_reduce(blk[:, 1:2], before_nb[:, :], AX.X, ALU.add).then_inc(t_v, 1)
            nc.vector.tensor_scalar(blk[:, 2:3], blk[:, 0:1], float(REGION_BLOCKS), slot_id, ALU.mult, ALU.add).then_inc(t_v, 1)
            nc.vector.tensor_scalar(table_f[:, 1:2], blk[:, 0:1], float(EXPERTS - 1), float(F_EXP), ALU.min, ALU.mult)
            dve.wait_ge(t_v, 5)
            nc.vector.tensor_scalar(table_f[:, 0:1], blk[:, 2:3], blk[:, 1:2], float(EXPERTS * REGION_BLOCKS),
                                    ALU.subtract, ALU.min).then_inc(t_tab, 1)
            shared_h(1, 1)
            shared_add(0)
            dve.wait_ge(t_row, 1)
            nc.vector.tensor_copy(table_b[0:1, LEAD:], pZ[0:1, P:2 * P])
            nc.vector.tensor_copy(table_e[0:1, LEAD:], pZ[0:1, 2 * P:3 * P]).then_inc(t_table, 1)

            for i in range(1, AHEAD):
                if i + 1 < AHEAD:
                    shared_h(i + 1, (i + 1) % 2)
                if i + 1 < AHEAD:
                    shared_add(i)

            def body(it, first):
                for j in range(BODY):
                    n = it * BODY + j
                    if not first and j == 6:
                        shared_h(it + (AHEAD - 1))
                    if j == (3 if first else 9):
                        shared_add(it + (AHEAD - 1))
                    if not (first and j < 2):
                        hidden(n - 2, (j - 2) % BODY)
                    transposed(n, j, hid=not (first and j < 3))

            body(0, True)
            with dve.Fori(1, TURNS) as it:
                body(it, False)
            for k in range(3):
                if k < 2:
                    hidden(BLOCKS - 2 + k, BODY - 2 + k)
                transposed(BLOCKS + k, k, rows=False)

            def total(q):
                dve.wait_ge(c_sum, q + 1)
                dve.wait_ge(h_add, 2 * q + 2)
                nc.vector.tensor_tensor(quad(X1, q), quad(X1, q), ysum[:, q, :], ALU.add).then_inc(c_out, 1)

            def due(k):
                return min(NQ, max(0, k - 1) + max(0, k - 4))

            for i in range(AFTER, HALVES):
                shared_h(i, i % 2)
                if i > AFTER:
                    shared_add(i - 1)
                k = i - AFTER
                for q in range(due(k - 1), due(k)):
                    total(q)
            shared_add(HALVES - 1)
            for q in range(due(HALVES - 1 - AFTER), NQ):
                total(q)

        @block.tensor
        def _(pe):
            pe.wait_ge(s_ones, 2)
            pe.wait_ge(s_bo, 16)
            pe.wait_ge(s_cn, 16)
            pe.wait_ge(s_wa, 16)

            def shared_gu_part(i, part, pair=0):
                f, w0, bank = part // 2, (F_SG, F_SU)[part % 2], (pSG, pSU)[part % 2][pair]
                if part == 0:
                    wait(pe, h_h, i - 1 if isinstance(i, int) else i)
                l = nc.tensor.matmul(bank[:, f * HALF:(f + 1) * HALF], WF[:, w0 + f * P:w0 + (f + 1) * P],
                                     ZT[:, bass.ds(i * HALF, HALF)], start=True, stop=True)
                if part == 3:
                    l.then_inc(h_gu, 1)

            def shared_d_part(i, t):
                if t == 0:
                    pe.wait_ge(h_h, i + 1)
                    wait(pe, h_add, i)
                for f in range(2):
                    l = nc.tensor.matmul(pSD[:, t * D:(t + 1) * D],
                                         sh_h[:, f * HALF + t * P:f * HALF + (t + 1) * P],
                                         WF[:, F_SD + f * D:F_SD + (f + 1) * D], start=(f == 0), stop=(f == 1))
                if t == 1:
                    l.then_inc(h_d, 1)

            def shared_gu(i):
                for part in range(4):
                    shared_gu_part(i, part, i % 2)

            def shared_d(i):
                for t in range(2):
                    shared_d_part(i, t)

            def tokens_t(q, par):
                pe.wait_ge(a_norm, q + 1)
                wait(pe, a_xT, q)
                for t in range(QUAD):
                    i = nc.tensor.transpose(pT[:, t * P:(t + 1) * P], XN[:, par, t, :], ident)
                i.then_inc(a_T, 1)

            def step(s, par):
                other = 1 - par
                if has(s, 1):
                    q = s - 1
                    pe.wait_ge(a_kf, q + 1)
                    pe.wait_ge(a_v, q + 1)
                    wait(pe, b_aT, q)
                    for b in range(SPQ):
                        for j in range(2):
                            i = nc.tensor.matmul(pKV[:, b, 0:D + 1], KF[:, other, 2 * b + j, :],
                                                 V[:, other, 2 * b + j, 0:D + 1], start=(j == 0), stop=(j == 1))
                    i.then_inc(b_kv, 1)
                if has(s, 0):
                    pe.wait_ge(a_xT, s + 1)
                    wait(pe, a_qf, s)
                    nc.tensor.matmul(pQ[:, :], WA[:, W_Q:W_Q + D], XNT[:, par, :], start=True, stop=True).then_inc(a_q, 1)
                if has(s, 3):
                    q = s - 3
                    pe.wait_ge(c_ch, q + 1)
                    wait(pe, c_cha, q)
                    nc.tensor.matmul(pR, tri[:, :], chosen[:, :, :], start=True, stop=False)
                    for t in range(QUAD - 1):
                        nc.tensor.matmul(pR[:, t + 1:QUAD, :], ones[:, :],
                                         chosen[:, t:t + 1, :].to_broadcast([P, QUAD - 1 - t, EXPERTS]),
                                         start=False, stop=False)
                    nc.tensor.matmul(pR, ones[:, :], chosen_all[:, :].unsqueeze(1).to_broadcast([P, QUAD, EXPERTS]),
                                     start=False, stop=True).then_inc(c_rank, 1)
                if has(s, 1):
                    q = s - 1
                    pe.wait_ge(a_qf, q + 1)
                    pe.wait_ge(b_mask, q + 1)
                    wait(pe, b_att, q)
                    wait(pe, c_x1, q)
                    for t in range(QUAD):
                        i = nc.tensor.matmul(pN[:, t, 0:RK], QF[:, other, t * P:(t + 1) * P], KV[:, t // 2, :],
                                             start=True, stop=True)
                    i.then_inc(b_num, 1)
                if has(s, 0):
                    wait(pe, a_kf, s)
                    wait(pe, a_v, s)
                    for t in range(QUAD):
                        i = nc.tensor.matmul(pKVN[:, t, :], XNT[:, par, t * P:(t + 1) * P], WA[:, W_KV:W_KV + 2 * D],
                                             start=True, stop=True)
                    i.then_inc(a_kv, 1)
                if final(s):
                    pe.wait_ge(c_x1, NQ)
                    pe.wait_ge(s_wf, 16)
                    pe.wait_ge(c_zT2, 1)
                    shared_gu(0)
                if has(s, 2):
                    q = s - 2
                    pe.wait_ge(c_z, q + 1)
                    wait(pe, c_slot, q)
                    for t in range(QUAD):
                        i = nc.tensor.transpose(pZ[:, t * P:(t + 1) * P], Z[:, par, t, 0, 0:D], ident)
                    i.then_inc(c_T, 1)
                if has(s, 1):
                    q = s - 1
                    pe.wait_ge(b_att, q + 1)
                    for t in range(QUAD):
                        i = nc.tensor.transpose(pAT[:, t * P:(t + 1) * P], att[:, t, :], ident)
                    i.then_inc(b_T, 1)
                if has(s, 2):
                    q = s - 2
                    pe.wait_ge(c_zT, q + 1)
                    for t in range(QUAD):
                        i = nc.tensor.matmul(pL[:, t, :], zT[:, t * P:(t + 1) * P], WA[:, W_R:W_R + EXPERTS],
                                             start=True, stop=True)
                    i.then_inc(c_lg, 1)
                if has(s, 1):
                    q = s - 1
                    pe.wait_ge(b_aT, q + 1)
                    for t in range(QUAD):
                        i = nc.tensor.matmul(pO[:, t * P:(t + 1) * P], attT[:, t * P:(t + 1) * P], WA[:, W_O:W_O + D],
                                             start=True, stop=True)
                    i.then_inc(b_wo, 1)
                if has(s, -1):
                    tokens_t(s + 1, other)

            nc.tensor.matmul(pQ[:, 0:D], ones_row[0:1, :], bo_row[0:1, :], start=True, stop=True).then_inc(s_bo_all, 1)
            tokens_t(0, 0)
            pe.wait_ge(s_tri, 1)
            pe.wait_ge(s_bo_all, 2)
            steps(pe, step)

            def transposes(n, it, j, rows=True, hid=True):
                if rows and j % 2 == 0:
                    pe.wait_ge(xs[j // 2], it * 32 + 32)
                wait(pe, s_xhT, n)
                if rows:
                    i = nc.tensor.transpose(pXH[:, 0, :], XS[:, j, 0:D], ident)
                if hid:
                    pe.wait_ge(s_h, n - 2)
                    i = nc.tensor.transpose(pXH[:, 1, :], h[:, (j - 3) % 2, :], ident)
                i.then_inc(s_T, 1)

            def gate_up(n, j, w):
                nc.tensor.matmul(pGU[j % 2][:, 0:2 * EXP_DIM], xhT[:, j % 2, 0, :],
                                 WF[:, bass.ds(w, 2 * EXP_DIM)], start=True, stop=True).then_inc(s_gu, 1)

            def down(n, j, w):
                wait(pe, s_y, n)
                nc.tensor.matmul(pY, xhT[:, (j + 3) % 2, 1, :], WF[:, 2 * EXP_DIM:][:, bass.ds(w, D)],
                                 start=True, stop=True).then_inc(s_D, 1)

            def body(it, first):
                w = values(pe, table_e, it * BODY, BODY + LEAD, (EXPERTS - 1) * F_EXP)
                for j in range(BODY):
                    n = it * BODY + j
                    if not first and 1 <= j <= 4:
                        shared_gu_part(it + (AHEAD - 1), j - 1)
                    if (1 <= j <= 2) if first else (7 <= j <= 8):
                        shared_d_part(it + (AHEAD - 1), j - (1 if first else 7))
                    transposes(n, it, j, hid=not (first and j < 3))
                    if not (first and j < 1):
                        gate_up(n - 1, (j - 1) % BODY, w[j - 1 + LEAD])
                    if not (first and j < 4):
                        down(n - 4, (j - 4) % BODY, w[j - 4 + LEAD])

            pe.wait_ge(c_cha, NQ)
            pe.wait_ge(c_slot, NQ)
            nc.tensor.matmul(pZ[0:EXPERTS, 0:P], chosen_all[:, :], ones[:, :], start=True, stop=True)
            nc.tensor.matmul(pZ[0:1, 256:256 + EXPERTS], ones[:, 0:1], chosen_all[:, :], start=True, stop=True).then_inc(t_cnt, 1)
            pe.wait_ge(c_zT2, NQ)
            shared_gu(1)
            pe.wait_ge(t_nb, 1)
            pe.wait_ge(t_pad, 2)
            nc.tensor.matmul(pZ[:, 0:2 * EXPERTS], nb[:, :], CN[0:EXPERTS, C_CUM:C_CUM + 2 * EXPERTS],
                             start=True, stop=True).then_inc(t_cum, 1)
            shared_d(0)
            shared_gu(2)
            pe.wait_ge(t_tab, 1)
            for a in range(2):
                i = nc.tensor.matmul(pZ[0:1, 128 + a * P:128 + (a + 1) * P], table_f[:, a:a + 1], ident, start=True, stop=True)
            i.then_inc(t_row, 1)

            for i in range(1, AHEAD - 1):
                shared_d(i)
                if i + 2 < AHEAD:
                    shared_gu(i + 2)
            pe.wait_ge(t_table, 2)
            body(0, True)
            with pe.Fori(1, TURNS) as it:
                body(it, False)
            w = values(pe, table_e, BLOCKS, LEAD, (EXPERTS - 1) * F_EXP)
            for k in range(4):
                if k < 3:
                    transposes(BLOCKS + k, 0, k, rows=False)
                else:
                    pe.wait_ge(s_xhT, BLOCKS + k)
                if k == 0:
                    gate_up(BLOCKS - 1, BODY - 1, w[LEAD - 1])
                down(BLOCKS - 4 + k, BODY - 4 + k, w[LEAD - 4 + k])

            pe.wait_ge(h_h, AFTER)
            shared_gu(AFTER)
            shared_gu(AFTER + 1)
            for i in range(AFTER, HALVES):
                shared_d(i)
                if i + 2 < HALVES:
                    shared_gu(i + 2)


def kernel(L0_attn_x, L0_attn_wq, L0_attn_wk, L0_attn_wv, L0_attn_wo, L0_attn_bo, L0_ffn_router_w,
           L0_ffn_gate_up_w, L0_ffn_down_w, L0_ffn_shared_gate_w, L0_ffn_shared_up_w, L0_ffn_shared_down_w):
    import numpy as np
    import concourse.bacc as bacc
    from concourse.bass_utils import run_bass_kernel_spmd

    f32 = np.float32
    t = lambda a: np.asarray(a).T
    w_att = np.ascontiguousarray(np.concatenate(
        [t(L0_attn_wq), t(L0_attn_wk), t(L0_attn_wv), t(L0_attn_wo), t(L0_ffn_router_w)], axis=1))
    experts = np.concatenate([np.asarray(L0_ffn_gate_up_w), np.asarray(L0_ffn_down_w)], axis=2)
    experts = experts.transpose(1, 0, 2).reshape(P, -1)
    s_down = t(L0_ffn_shared_down_w).reshape(SHARED // P, P, D).transpose(1, 0, 2).reshape(P, -1)
    w_ffn = np.ascontiguousarray(np.concatenate(
        [experts, t(L0_ffn_shared_gate_w), t(L0_ffn_shared_up_w), s_down], axis=1))
    i, c = np.arange(P)[:, None], np.arange(P)[None, :]
    e = np.arange(EXPERTS)[None, :]
    consts = np.zeros((P, C_ALL), f32)
    consts[:, C_IDENT:C_IDENT + P] = i == c
    consts[:, C_TRI:C_TRI + P] = i < c
    consts[:, C_MASK:C_MASK + D] = i // HD == c // HD
    consts[:, C_MASK + D:C_MASK + RK] = i // HD == e
    consts[:, C_IOTA:C_IOTA + EXPERTS] = e
    consts[:, C_BASE:C_BASE + EXPERTS] = e * REGION
    consts[:, C_SLOT:C_SLOT + 1] = i
    consts[0:EXPERTS, C_CUM:C_CUM + EXPERTS] = i[:EXPERTS] <= e
    consts[0:EXPERTS, C_CUM + EXPERTS:C_ALL] = i[:EXPERTS] == e
    q, b, j, k = np.meshgrid(np.arange(NQ), np.arange(SPQ), np.arange(2), np.arange(TOP_K), indexing="ij")
    tokid = (k * TOKENS + q * QTOK + b * SEQ + j).reshape(1, -1) + 2 * i
    arrays = {
        "x": np.ascontiguousarray(np.asarray(L0_attn_x).reshape(TOKENS, D)),
        "w_att": w_att,
        "bo": np.ascontiguousarray(np.asarray(L0_attn_bo).reshape(1, D)),
        "w_ffn": w_ffn,
        "consts": consts,
        "tokid": tokid.astype(np.uint32),
    }
    nc = bacc.Bacc("TRN2", target_bir_lowering=False, num_devices=1)
    args = [nc.dram_tensor(n, a.shape, mybir.dt.from_np(a.dtype), kind="ExternalInput").ap() for n, a in arrays.items()]
    out = nc.dram_tensor("out", (TOKENS, D), mybir.dt.float32, kind="ExternalOutput").ap()
    preln_block(nc, *args, out)
    r = run_bass_kernel_spmd(nc, [arrays], core_ids=[0])
    return r.results[0]["out"].reshape(BATCHES, SEQ, D)
```
